# Optimizing a Trainium2 kernel written in Bass

```python
import numpy as np
import jax
import jax.numpy as jnp

def _softmax(x, axis=-1):
    return jax.nn.softmax(x, axis=axis)
def _gelu(x):
    return jax.nn.gelu(x, approximate=True)
def _silu(x):
    return jax.nn.silu(x)
def _sigmoid(x):
    return jax.nn.sigmoid(x)
def _layernorm(x, axis=-1, eps=1e-5):
    m = jnp.mean(x, axis=axis, keepdims=True)
    v = jnp.var(x, axis=axis, keepdims=True)
    return (x - m) / jnp.sqrt(v + eps)
def _scatter_add(tgt, idx, src, axis=0):
    return tgt.at[idx].add(src)
def _segment_sum(src, seg, n):
    return jax.ops.segment_sum(src, seg, n)

kernel_name = 'mk_conv_seq_d2_conv_nchw96_d1e003'

def setup_inputs(seed: int = 0):
    np.random.seed(seed)
    _w = jnp.asarray
    def _rec_inputs():
        import jax
        import jax.numpy as jnp
        _gk = jax.random.key(seed)
        x = -0.0001538 + 1 * jax.random.normal(jax.random.fold_in(_gk, 1), (16, 96, 64, 64), jnp.float32)
        return x
    x = _rec_inputs()
    def _L0_conv_setup():
        import jax, jax.numpy as jnp
        import numpy as np
        WS = 8
        K = 9
        BN_EPS = 1e-05

        def conv1x1(x, w, b):
            return jnp.einsum('bchw,oc->bohw', x, w) + b[None, :, None, None]

        def affine(x, s, t):
            return x * s[None, :, None, None] + t[None, :, None, None]

        def window_partition(x, ws):
            B, C, H, W = x.shape
            x = x.reshape(B, C, H // ws, ws, W // ws, ws)
            x = x.transpose(0, 2, 4, 1, 3, 5)
            return x.reshape(-1, C, ws, ws)

        def window_reverse(win, ws, B, H, W):
            C = win.shape[1]
            x = win.reshape(B, H // ws, W // ws, C, ws, ws)
            x = x.transpose(0, 3, 1, 4, 2, 5)
            return x.reshape(B, C, H, W)

        def knn_idx(nodes, k):
            nrm = jnp.maximum(jnp.linalg.norm(nodes, axis=-1, keepdims=True), 1e-12)
            xn = nodes / nrm
            sq = jnp.sum(xn * xn, axis=-1, keepdims=True)
            dist = sq - 2.0 * jnp.einsum('bnc,bmc->bnm', xn, xn) + sq.transpose(0, 2, 1)
            _, idx = jax.lax.top_k(-dist, k)
            return idx
        key = jax.random.key(seed)
        ks = jax.random.split(key, 16)
        B, C, H, W = (16, 96, 64, 64)
        O = 2 * C

        def bn(k1, k2, n):
            g = 1.0 + 0.1 * jax.random.normal(k1, (n,), jnp.float32)
            b = 0.1 * jax.random.normal(k2, (n,), jnp.float32)
            return (g, b)
        x = jax.random.normal(ks[0], (B, C, H, W), jnp.float32)
        fc1_w = 0.05 * jax.random.normal(ks[1], (C, C), jnp.float32)
        fc1_b = 0.02 * jax.random.normal(ks[2], (C,), jnp.float32)
        fc1_s, fc1_t = bn(ks[3], ks[4], C)
        ew = 0.05 * jax.random.normal(ks[5], (O, 2 * C), jnp.float32)
        eb = 0.02 * jax.random.normal(ks[6], (O,), jnp.float32)
        es, et = bn(ks[7], ks[8], O)
        fc2_w = 0.05 * jax.random.normal(ks[9], (C, O), jnp.float32)
        fc2_b = 0.02 * jax.random.normal(ks[10], (C,), jnp.float32)
        fc2_s, fc2_t = bn(ks[11], ks[12], C)
        return {'x': x, 'fc1_w': fc1_w, 'fc1_b': fc1_b, 'fc1_s': fc1_s, 'fc1_t': fc1_t, 'ew': ew, 'eb': eb, 'es': es, 'et': et, 'fc2_w': fc2_w, 'fc2_b': fc2_b, 'fc2_s': fc2_s, 'fc2_t': fc2_t}
    _L0_conv_all = _L0_conv_setup()
    _L0_conv_in = {k: v for k, v in _L0_conv_all.items() if k in ('fc1_w', 'fc1_b', 'fc1_s', 'fc1_t', 'ew', 'eb', 'es', 'et', 'fc2_w', 'fc2_b', 'fc2_s', 'fc2_t', )}
    del _L0_conv_all

    def _L1_conv_setup():
        import jax, jax.numpy as jnp
        import numpy as np
        B, C, H, W = (64, 96, 56, 56)
        HID, OUP = (576, 96)
        EPS = 1e-05

        def _bn(x, g, b, m, v):
            scale = (g * jax.lax.rsqrt(v + EPS)).reshape(1, -1, 1, 1)
            shift = (b - m * g * jax.lax.rsqrt(v + EPS)).reshape(1, -1, 1, 1)
            return x * scale + shift
        key = jax.random.key(seed)
        ks = jax.random.split(key, 16)
        n = lambda k, s, sc=1.0: jax.random.normal(k, s, dtype=jnp.float32) * sc
        u = lambda k, s: jax.random.uniform(k, s, dtype=jnp.float32, minval=0.5, maxval=1.5)
        return {'x': n(ks[0], (B, C, H, W)), 'w1': n(ks[1], (HID, C), 0.05), 'g1': u(ks[2], (HID,)), 'b1': n(ks[3], (HID,), 0.1), 'm1': n(ks[4], (HID,), 0.1), 'v1': u(ks[5], (HID,)), 'wd': n(ks[6], (HID, 1, 3, 3), 0.05), 'gd': u(ks[7], (HID,)), 'bd': n(ks[8], (HID,), 0.1), 'md': n(ks[9], (HID,), 0.1), 'vd': u(ks[10], (HID,)), 'w2': n(ks[11], (OUP, HID), 0.05), 'g2': u(ks[12], (OUP,)), 'b2': n(ks[13], (OUP,), 0.1), 'm2': n(ks[14], (OUP,), 0.1), 'v2': u(ks[15], (OUP,))}
    _L1_conv_all = _L1_conv_setup()
    _L1_conv_in = {k: v for k, v in _L1_conv_all.items() if k in ('w1', 'g1', 'b1', 'm1', 'v1', 'wd', 'gd', 'bd', 'md', 'vd', 'w2', 'g2', 'b2', 'm2', 'v2', )}
    del _L1_conv_all

    return {
        "x": x,
        "L0_conv_fc1_w": _L0_conv_in["fc1_w"],
        "L0_conv_fc1_b": _L0_conv_in["fc1_b"],
        "L0_conv_fc1_s": _L0_conv_in["fc1_s"],
        "L0_conv_fc1_t": _L0_conv_in["fc1_t"],
        "L0_conv_ew": _L0_conv_in["ew"],
        "L0_conv_eb": _L0_conv_in["eb"],
        "L0_conv_es": _L0_conv_in["es"],
        "L0_conv_et": _L0_conv_in["et"],
        "L0_conv_fc2_w": _L0_conv_in["fc2_w"],
        "L0_conv_fc2_b": _L0_conv_in["fc2_b"],
        "L0_conv_fc2_s": _L0_conv_in["fc2_s"],
        "L0_conv_fc2_t": _L0_conv_in["fc2_t"],
        "L1_conv_w1": _L1_conv_in["w1"],
        "L1_conv_g1": _L1_conv_in["g1"],
        "L1_conv_b1": _L1_conv_in["b1"],
        "L1_conv_m1": _L1_conv_in["m1"],
        "L1_conv_v1": _L1_conv_in["v1"],
        "L1_conv_wd": _L1_conv_in["wd"],
        "L1_conv_gd": _L1_conv_in["gd"],
        "L1_conv_bd": _L1_conv_in["bd"],
        "L1_conv_md": _L1_conv_in["md"],
        "L1_conv_vd": _L1_conv_in["vd"],
        "L1_conv_w2": _L1_conv_in["w2"],
        "L1_conv_g2": _L1_conv_in["g2"],
        "L1_conv_b2": _L1_conv_in["b2"],
        "L1_conv_m2": _L1_conv_in["m2"],
        "L1_conv_v2": _L1_conv_in["v2"],
    }

def reference(x, L0_conv_fc1_w, L0_conv_fc1_b, L0_conv_fc1_s, L0_conv_fc1_t, L0_conv_ew, L0_conv_eb, L0_conv_es, L0_conv_et, L0_conv_fc2_w, L0_conv_fc2_b, L0_conv_fc2_s, L0_conv_fc2_t, L1_conv_w1, L1_conv_g1, L1_conv_b1, L1_conv_m1, L1_conv_v1, L1_conv_wd, L1_conv_gd, L1_conv_bd, L1_conv_md, L1_conv_vd, L1_conv_w2, L1_conv_g2, L1_conv_b2, L1_conv_m2, L1_conv_v2):
    import jax
    import jax.numpy as jnp
    def _L0_conv_ref(x, fc1_w, fc1_b, fc1_s, fc1_t, ew, eb, es, et, fc2_w, fc2_b, fc2_s, fc2_t):
        import jax, jax.numpy as jnp
        import numpy as np
        WS = 8
        K = 9
        BN_EPS = 1e-05

        def conv1x1(x, w, b):
            return jnp.einsum('bchw,oc->bohw', x, w) + b[None, :, None, None]

        def affine(x, s, t):
            return x * s[None, :, None, None] + t[None, :, None, None]

        def window_partition(x, ws):
            B, C, H, W = x.shape
            x = x.reshape(B, C, H // ws, ws, W // ws, ws)
            x = x.transpose(0, 2, 4, 1, 3, 5)
            return x.reshape(-1, C, ws, ws)

        def window_reverse(win, ws, B, H, W):
            C = win.shape[1]
            x = win.reshape(B, H // ws, W // ws, C, ws, ws)
            x = x.transpose(0, 3, 1, 4, 2, 5)
            return x.reshape(B, C, H, W)

        def knn_idx(nodes, k):
            nrm = jnp.maximum(jnp.linalg.norm(nodes, axis=-1, keepdims=True), 1e-12)
            xn = nodes / nrm
            sq = jnp.sum(xn * xn, axis=-1, keepdims=True)
            dist = sq - 2.0 * jnp.einsum('bnc,bmc->bnm', xn, xn) + sq.transpose(0, 2, 1)
            _, idx = jax.lax.top_k(-dist, k)
            return idx
        B, C, H, W = x.shape
        tmp = x
        y = affine(conv1x1(x, fc1_w, fc1_b), fc1_s, fc1_t)
        win = window_partition(y, WS)
        Bw = win.shape[0]
        nodes = win.reshape(Bw, C, WS * WS).transpose(0, 2, 1)
        idx = jax.lax.stop_gradient(knn_idx(nodes, K))
        x_j = jax.vmap(lambda n, i: n[i])(nodes, idx)
        x_i = nodes[:, :, None, :]
        feat = jnp.concatenate([jnp.broadcast_to(x_i, x_j.shape), x_j - x_i], axis=-1)
        h = jnp.einsum('bnkc,oc->bnko', feat, ew) + eb
        h = h * es + et
        h = jax.nn.gelu(h, approximate=False)
        h = jnp.max(h, axis=2)
        O = h.shape[-1]
        win_out = h.transpose(0, 2, 1).reshape(Bw, O, WS, WS)
        y = window_reverse(win_out, WS, B, H, W)
        y = affine(conv1x1(y, fc2_w, fc2_b), fc2_s, fc2_t)
        return y + tmp

    def _L1_conv_ref(x, w1, g1, b1, m1, v1, wd, gd, bd, md, vd, w2, g2, b2, m2, v2):
        import jax, jax.numpy as jnp
        import numpy as np
        B, C, H, W = (64, 96, 56, 56)
        HID, OUP = (576, 96)
        EPS = 1e-05

        def _bn(x, g, b, m, v):
            scale = (g * jax.lax.rsqrt(v + EPS)).reshape(1, -1, 1, 1)
            shift = (b - m * g * jax.lax.rsqrt(v + EPS)).reshape(1, -1, 1, 1)
            return x * scale + shift
        h = jnp.einsum('oc,bchw->bohw', w1, x)
        h = jax.nn.relu(_bn(h, g1, b1, m1, v1))
        h = jax.lax.conv_general_dilated(h, wd, window_strides=(1, 1), padding=((1, 1), (1, 1)), feature_group_count=HID, dimension_numbers=('NCHW', 'OIHW', 'NCHW'))
        h = jax.nn.relu(_bn(h, gd, bd, md, vd))
        h = jnp.einsum('oc,bchw->bohw', w2, h)
        h = _bn(h, g2, b2, m2, v2)
        return x + h

    def _gn(v, G=32, eps=1e-5):
        B_, C_, H_, W_ = v.shape
        g = v.reshape(B_, G, C_ // G, H_, W_)
        m = jnp.mean(g, axis=(2, 3, 4), keepdims=True)
        s = jnp.var(g, axis=(2, 3, 4), keepdims=True)
        return ((g - m) / jnp.sqrt(s + eps)).reshape(v.shape)

    def _ln_c(v, eps=1e-6):
        m = jnp.mean(v, axis=1, keepdims=True)
        s = jnp.var(v, axis=1, keepdims=True)
        return (v - m) / jnp.sqrt(s + eps)

    def _ln_t(v, eps=1e-5):
        m = jnp.mean(v, axis=-1, keepdims=True)
        s = jnp.var(v, axis=-1, keepdims=True)
        return (v - m) / jnp.sqrt(s + eps)

    def _to_tokens(v):
        B_, C_, H_, W_ = v.shape
        return v.reshape(B_, C_, H_ * W_).transpose(0, 2, 1)
    def _from_tokens(t, like):
        B_, C_, H_, W_ = like.shape
        return t.transpose(0, 2, 1).reshape(B_, C_, H_, W_)

    x = _L0_conv_ref(x, L0_conv_fc1_w, L0_conv_fc1_b, L0_conv_fc1_s, L0_conv_fc1_t, L0_conv_ew, L0_conv_eb, L0_conv_es, L0_conv_et, L0_conv_fc2_w, L0_conv_fc2_b, L0_conv_fc2_s, L0_conv_fc2_t)
    x = _L1_conv_ref(x, L1_conv_w1, L1_conv_g1, L1_conv_b1, L1_conv_m1, L1_conv_v1, L1_conv_wd, L1_conv_gd, L1_conv_bd, L1_conv_md, L1_conv_vd, L1_conv_w2, L1_conv_g2, L1_conv_b2, L1_conv_m2, L1_conv_v2)
    return x


_drawn_inputs = setup_inputs


def setup_inputs(seed=0):
    import zlib

    import numpy as np

    out = dict(_drawn_inputs(seed))
    spreads = {}
    factors = {'L0_conv_fc1_b': 3.745,
     'L0_conv_eb': 5.294,
     'L0_conv_fc2_b': 2.845,
     'L1_conv_g1': 47.345,
     'L1_conv_b1': 20.315,
     'L1_conv_m1': 6.809,
     'L1_conv_v1': 152.198,
     'L1_conv_vd': 67.564,
     'L1_conv_gd': 2.932}
    for name, (base, spread) in spreads.items():
        noise = np.random.default_rng([zlib.crc32(name.encode()), seed]).standard_normal(out[name].shape)
        drawn = base * np.exp(spread * noise) if base else spread * noise
        out[name] = jnp.asarray(drawn.astype(out[name].dtype))
    for name, factor in factors.items():
        out[name] = (out[name] * factor).astype(out[name].dtype)
    return out
```

```python
import concourse.bass as bass
from concourse import mybir
from contextlib import ExitStack

B, C, H, W = 16, 96, 64, 64
WS = 8
NODES = WS * WS
O = 2 * C
KN = 8
HID = 576
FULL, HALF = HID // 128, HID % 128
PAIRS = (H // WS) * (W // WS) // 2
CHUNKS = H // WS
PPC = PAIRS // CHUNKS
CW = WS * W
STRIP = 16
STRIPS = H // STRIP
SLOTS = PAIRS // STRIPS
TAPS = 9
PADW = W + 2
ONE128 = 128
NPAIRS, NSTRIPS = B * PAIRS, B * STRIPS


def valid(v, n):
    return not isinstance(v, int) or 0 <= v < n


def misc_jobs(b, p):
    t, i = p // SLOTS, p % SLOTS
    jobs = []
    half = p // 16
    bi = b + half
    c0 = 4 if half == 0 else 0
    q = p % 16
    if valid(bi, B):
        if 1 <= q <= 4:
            jobs.append(("fc1", bi, c0 + q - 1))
        if 2 <= q <= 5:
            jobs.append(("ssq", bi, c0 + q - 2))
        if 9 <= q <= 12:
            jobs.append(("inv", bi, c0 + q - 9))
    if p % 4 == 1:
        bc, c = (b, (p - 5) // 4) if p >= 5 else (b - 1, CHUNKS - 1)
        if valid(bc, B):
            jobs.append(("fc2", bc, c))
    s = STRIPS * b + t - 2
    if valid(s, NSTRIPS) and i <= FULL:
        jobs += [("w1", s, i, m) for m in range(3 if i < FULL else 2)]
    if valid(s - 1, NSTRIPS) and i >= 4:
        jobs.append(("w2", s - 1, i - 4))
    return jobs


def jobs_in(b, upto=PAIRS):
    return sum(len(misc_jobs(b, p)) for p in range(16 if b < 0 else 0, upto))


PER_IMAGE = jobs_in(1)
BEFORE = {-1: 0, 0: jobs_in(-1)}
BEFORE[1] = BEFORE[0] + jobs_in(0)
for _b in range(2, B):
    BEFORE[_b] = BEFORE[1] + (_b - 1) * PER_IMAGE
BEFORE[B] = BEFORE[B - 1] + jobs_in(B - 1)


def jobs_before(b):
    return BEFORE[b] if isinstance(b, int) else BEFORE[1] + (b - 1) * PER_IMAGE


def job_at(b, p, kind, which):
    n = 0
    for pp in range(16 if isinstance(b, int) and b < 0 else 0, PAIRS):
        for j in misc_jobs(b, pp):
            n += 1
            if pp == p and j[0] == kind and j[-1] == which and (kind != "w1" or j[2] == p % SLOTS):
                return jobs_before(b) + n
    raise AssertionError((b, p, kind, which))


def bank_of(b, p, k):
    if not isinstance(b, int):
        b = 1
    return (jobs_before(b) + jobs_in(b, p) + k) % 2


def when(b, p, ago):
    p -= ago
    return (b, p) if p >= 0 else (b - 1, p + PAIRS)


def taps_of(i):
    first = [(g, k) for k in range(TAPS) for g in (0, 1)]
    second = [(g, k) for k in range(TAPS) for g in (2, 3, 4)]
    mine = {2: first[0:6], 3: first[6:12], 4: first[12:18],
            5: second[0:6], 6: second[6:12], 7: second[12:17]}.get(i, [])
    previous = {0: second[17:22], 1: second[22:27]}.get(i, [])
    return mine, previous


def tap_number(s, g, k):
    return s * (5 * TAPS) + (2 * k + g if g < 2 else 2 * TAPS + 3 * k + g - 2) + 1


def due(count):
    return not isinstance(count, int) or count > 0


def build(nc, x, p97, p128, rows97, consts, consts128, consts16, out):
    f32, f16, u32 = mybir.dt.float32, mybir.dt.float16, mybir.dt.uint32
    ALU, ACT, AX = mybir.AluOpType, mybir.ActivationFunctionType, mybir.AxisListType
    ctx = ExitStack()
    with ctx:
        def sb(name, shape, dt=f32):
            return ctx.enter_context(nc.sbuf_tensor(name, shape, dt))

        def pb(name, shape):
            return ctx.enter_context(nc.psum_tensor(name, shape, f32))

        def sem(name):
            return ctx.enter_context(nc.semaphore(name))

        w97 = sb("w97", [C + 1, P97])
        w128 = sb("w128", [128, P128])
        cst = sb("cst", [128, CF])
        ones = sb("ones", [C, 1])
        onesq = sb("onesq", [128, 4 * PPC, C + 1])
        eye128 = sb("eye128", [128, 128])
        c16 = sb("c16", [128, C16], f16)
        wVU = sb("wVU", [C + 1, 2, O])
        l0sc = sb("l0sc", [C, 2])
        bn = sb("bn", [128, 3, 5])
        sc1, sh1 = sb("sc1", [128, 5]), sb("sh1", [128, 5])
        scd, shd = sb("scd", [128, 5]), sb("shd", [128, 5])
        sc2 = sb("sc2", [C, 2])
        tmp2 = sb("tmp2", [C, 2])
        zrow = sb("zrow", [128, W])
        expo = sb("expo", [128, 1])

        def col97(k):
            return w97[0:C, k:k + 1]

        fc1T = w97[0:C, 0:C]
        w1T = w97[0:C, C:C + HID]
        V97 = C + HID
        fc2T = w128[:, 0:3 * C].rearrange("p (k c) -> p k c", k=3)
        w2T = w128[:, 3 * C:8 * C].rearrange("p (g c) -> p g c", g=5)
        wd = w128[:, 8 * C:8 * C + 45].rearrange("p (g k) -> p g k", g=5)
        bnp = w128[:, 8 * C + 45:8 * C + 85].rearrange("p (n g) -> p n g", n=8)
        nbias = cst[:, 0:1]
        maskw = cst[:, 1:17].rearrange("p (win k) -> p win k", win=2)
        onerow = cst[C:C + 1, 17:17 + NODES]
        eye = cst[:, 81:81 + NODES]
        I2 = c16[:, 0:NODES]
        Imask = c16[0:64, 64:128]
        negI = c16[0:64, 192:256]
        LK = c16[0:32, 256:256 + KN * 128].rearrange("p (k m) -> p k m", k=KN)

        xin = sb("xin", [C, 2, 4 * CW])
        xres = sb("xres", [C, 4, CW])
        y = sb("y", [C + 1, CHUNKS, CW])
        xn = sb("xn", [C + 1, CHUNKS, CW])
        ysq = sb("ysq", [C, 2, CW])
        ssq = sb("ssq", [128, 4 * PPC])
        clamped = sb("clamped", [128, 4 * PPC])
        inv = sb("inv", [128, 4 * PPC])
        sqn = sb("sqn", [128, 4 * PPC])
        diag = sb("diag", [128, 2, PPC, 128])
        invb = sb("invb", [C + 1, 2, CW])
        top8 = sb("top8", [128, 2, 8])
        idx = sb("idx", [128, 2, 8], u32)
        feat = sb("feat", [128, 2, 2, 2 * KN], f16)
        featT = sb("featT", [32, 2, NODES], f16)
        VU = sb("VU", [128, 2, 2, O])
        MV = sb("MV", [128, 2, 2, KN + 1, NODES])
        g = sb("g", [128, 2, 3, KN + 1, NODES])
        gflat = g[:, 0].rearrange("p c k n -> p (c k n)")
        c16f = gflat[:, 0:C16]
        r97 = g[0:C + 1, 1].rearrange("p c k n -> p (c k n)")[:, 0:3 * O]
        hid = sb("hid", [128, 2, PPC, 3, NODES])
        x1 = sb("x1", [C, H, W])
        hpad = sb("hpad", [128, 5, STRIP + 2, PADW])
        acc = sb("acc", [128, 2, 5, STRIP * W])
        res = sb("res", [C, 2, CW])

        pmisc = [pb(f"pmisc{k}", [128, 512]) for k in range(2)]
        pscore = pb("pscore", [128, 512])
        pself = pb("pself", [128, 512])
        pone = pb("pone", [128, KN, NODES])
        pvu = pb("pvu", [128, 512])
        pg = [pb(f"pg{k}", [128, 512]) for k in range(2)]

        param_load, consts_ready, bn_sqrt_in, bn_sqrt_out = (sem(n) for n in (
            "param_load", "consts_ready", "bn_sqrt_in", "bn_sqrt_out"))
        dve_setup, act_setup = sem("dve_setup"), sem("act_setup")
        xin_load = [sem(f"xin_load{k}") for k in range(2)]
        xres_load = [sem(f"xres_load{k}") for k in range(4)]
        store_done = [sem(f"store_done{k}") for k in range(2)]
        misc_ready, misc_evac = sem("misc_ready"), sem("misc_evac")
        ysq_ready, pool_step, inv_ready, diag_ready, xn_ready = (sem(n) for n in (
            "ysq_ready", "pool_step", "inv_ready", "diag_ready", "xn_ready"))
        score_ready, top8_ready, idx_ready, a_ready, feat_ready = (sem(n) for n in (
            "score_ready", "top8_ready", "idx_ready", "a_ready", "feat_ready"))
        featT_ready, featT_evac, onehot_in, onehot_ready = (sem(n) for n in (
            "featT_ready", "featT_evac", "onehot_in", "onehot_ready"))
        vu_ready, vu_evac, gather_ready, self_ready, gelu_done, self_gelu = (sem(n) for n in (
            "vu_ready", "vu_evac", "gather_ready", "self_ready", "gelu_done", "self_gelu"))
        sp_passed, pool_passed, dve_passed = sem("sp_passed"), sem("pool_passed"), sem("dve_passed")
        hid_ready, x1_ready, tap_done, relu_done, out_added = (sem(n) for n in (
            "hid_ready", "x1_ready", "tap_done", "relu_done", "out_added"))

        block = ctx.enter_context(nc.Block())

        def image_loop(eng, image, tail):
            image(-1, 16, PAIRS)
            image(0, 0, PAIRS)
            with eng.Fori(1, B - 1) as b:
                image(b, 0, PAIRS)
            image(B - 1, 0, PAIRS)
            image(B, 0, tail)

        @block.sync
        def _(sp):
            sp.dma_start(w97[:, :], p97).then_inc(param_load, 16)
            sp.dma_start(w128[:, :], p128).then_inc(param_load, 16)
            sp.dma_start(r97[:, :], rows97).then_inc(param_load, 16)
            sp.dma_start(cst[:, :], consts).then_inc(param_load, 16)
            sp.dma_start(eye128[:, :], consts128).then_inc(param_load, 16)
            sp.dma_start(c16f[:, :], consts16).then_inc(param_load, 16)
            xv = x.rearrange("b c row col -> b c (row col)")
            ov = out.rearrange("b c row col -> b c (row col)")

            def load_half(b, h):
                sp.dma_start(xin[:, h, :], xv[b, :, h * 4 * CW:(h + 1) * 4 * CW]).then_inc(xin_load[h], 16)

            def load_res(b, c):
                sp.dma_start(xres[:, c % 4, :], xv[b, :, c * CW:(c + 1) * CW]).then_inc(xres_load[c % 4], 16)

            load_half(0, 0)
            load_half(0, 1)

            def image(b, p0, p1):
                for p in range(p0, p1):
                    t, i = p // SLOTS, p % SLOTS
                    if p in (1, 6) and valid(b, B) and valid(b + 1, B):
                        h = p // 6
                        if due(count := CHUNKS * b + 4 * h + 4):
                            sp.wait_ge(ysq_ready, count)
                        sp.sem_inc(sp_passed, 1)
                        load_half(b + 1, h)
                    if isinstance(b, int) and b == -1 and p >= 28:
                        load_res(0, p - 28)
                    if p % 4 == 2:
                        bc, c = (b, (p - 6) // 4) if p >= 6 else (b - 1, CHUNKS - 1)
                        bl, cl = (bc, c + 4) if c < 4 else (bc + 1, c - 4)
                        if valid(bc, B) and valid(bl, B):
                            if due(count := CHUNKS * bc + c + 1):
                                sp.wait_ge(x1_ready, count)
                            sp.sem_inc(sp_passed, 1)
                            load_res(bl, cl)
                    for s, cc, at in ((STRIPS * b + t - 3, 0, 6), (STRIPS * b + t - 4, 1, 0)):
                        if i == at and valid(s, NSTRIPS):
                            if due(count := 2 * s + cc + 1):
                                sp.wait_ge(out_added, count)
                            sp.sem_inc(sp_passed, 1)
                            tt = (t - 3 if cc == 0 else t - 4) % STRIPS
                            bb = b - 1 if (t - 3 - cc) < 0 else b
                            c = 2 * tt + cc
                            sp.dma_start(ov[bb, :, c * CW:(c + 1) * CW], res[:, cc, :]).then_inc(store_done[cc], 16)

            image_loop(sp, image, TAIL)
            for k in range(2):
                sp.wait_ge(store_done[k], 16 * NSTRIPS)

        @block.gpsimd
        def _(pool):
            pool.wait_ge(consts_ready, 1)

            def inverse_norms(b, p, bi, h):
                n = 2 * bi + h
                fb, fp = when(b, p, 2)
                if due(count := job_at(fb, fp, "ssq", 4 * h + 3)):
                    pool.wait_ge(misc_evac, count)
                if due(count := 4 * n):
                    pool.wait_ge(diag_ready, count)
                pool.sem_inc(pool_passed, 1)
                nc.gpsimd.tensor_scalar(clamped[:, :], ssq[:, :], 1e-24, None, ALU.max).then_inc(pool_step, 1)
                pool.wait_ge(pool_step, 3 * n + 1)
                nc.gpsimd.tensor_tensor(inv[:, :], clamped[:, :], expo[:, 0:1].to_broadcast([128, 4 * PPC]),
                                        ALU.pow).then_inc(pool_step, 1)
                pool.wait_ge(pool_step, 3 * n + 2)
                nc.gpsimd.tensor_tensor(sqn[:, :], ssq[:, :], inv[:, :], ALU.mult).then_inc(pool_step, 1)
                pool.wait_ge(pool_step, 3 * n + 3)
                if due(count := 4 * n):
                    pool.wait_ge(xn_ready, count)
                pool.sem_inc(pool_passed, 1)
                nc.gpsimd.tensor_scalar(onesq[:, :, C], sqn[:, :], -0.5, None, ALU.mult).then_inc(inv_ready, 1)

            def image(b, p0, p1):
                for p in range(p0, p1):
                    if p % 16 == 7:
                        h = 1 if p == 7 else 0
                        bi = b if h else b + 1
                        if valid(bi, B):
                            inverse_norms(b, p, bi, h)

            image_loop(pool, image, TAIL)

        @block.tensor
        def _(pe):
            def shared_job(b, p, k, job):
                n = jobs_before(b) + jobs_in(b if isinstance(b, int) else 1, p) + k
                if due(count := n - 1):
                    pe.wait_ge(misc_evac, count)
                ps = pmisc[bank_of(b, p, k)]
                kind = job[0]
                if kind == "fc1":
                    bi, c = job[1:]
                    if c % 4 == 0:
                        if due(count := 16 * (bi + 1)):
                            pe.wait_ge(xin_load[c // 4], count)
                    last = nc.tensor.matmul(ps[0:C, :], fc1T, xin[:, c // 4, (c % 4) * CW:(c % 4 + 1) * CW],
                                            start=True, stop=True)
                elif kind == "ssq":
                    bi, c = job[1:]
                    if due(count := CHUNKS * bi + c + 1):
                        pe.wait_ge(ysq_ready, count)
                    for j in range(PPC):
                        last = nc.tensor.matmul(ps[:, j:j + 1], ysq[:, c % 2, j * 128:(j + 1) * 128], ones[:, :],
                                                start=True, stop=True)
                elif kind == "inv":
                    bi, c = job[1:]
                    if due(count := CHUNKS * bi + c + 1):
                        pe.wait_ge(diag_ready, count)
                    for j in range(PPC):
                        last = nc.tensor.matmul(ps[0:C + 1, j * 128:(j + 1) * 128], onesq[:, (c % 4) * PPC + j, :],
                                                diag[:, c % 2, j, :], start=True, stop=True)
                elif kind == "fc2":
                    bc, c = job[1:]
                    if due(count := PAIRS * bc + PPC * (c + 1)):
                        pe.wait_ge(hid_ready, count)
                    hc = hid[:, c % 2]
                    pw = ps[0:C, :].rearrange("p (q win n) -> p q win n", q=PPC, win=2)
                    for w in range(2):
                        nc.tensor.matmul(pw[:, :, w, :], fc2T[:, 1 + w, :], hc[:, :, 2, :], start=(w == 0),
                                         stop=False)
                    last = nc.tensor.matmul(ps[0:C, :].rearrange("p (q n) -> p q n", q=PPC), fc2T[:, 0, :],
                                            hc[:, :, 0:2, :].rearrange("p q win n -> p q (win n)"), start=False,
                                            stop=True)
                elif kind == "w1":
                    s, gr, m = job[1:]
                    t = (p // SLOTS - 2) % STRIPS
                    if gr == 0 and m == 0:
                        bs = b if p // SLOTS >= 2 else b - 1
                        if due(count := CHUNKS * bs + min(2 * t + 3, CHUNKS)):
                            pe.wait_ge(x1_ready, count)
                    top = STRIP * t - 1
                    if gr < FULL:
                        r0, r1 = 6 * m, 6 * m + 6
                        lo, hi = max(top + r0, 0), min(top + r1, H)
                        o = (lo - top - r0) * W
                        last = nc.tensor.matmul(ps[:, o:o + (hi - lo) * W], w1T[:, gr * 128:(gr + 1) * 128],
                                                x1[:, lo:hi, :], start=True, stop=True)
                    else:
                        for u in range(2):
                            first = top + 8 * u + 5 * m
                            lo, hi = max(first, 0), min(first + 5, H)
                            o = (lo - first) * W
                            last = nc.tensor.matmul(ps[64 * u:64 * u + 64, o:o + (hi - lo) * W],
                                                    w1T[:, FULL * 128:HID], x1[:, lo:hi, :], start=True, stop=True)
                else:
                    s, q = job[1:]
                    par = (p // SLOTS - 3) % 2
                    if q == 0:
                        if due(count := 5 * (s + 1)):
                            pe.wait_ge(relu_done, count)
                    for gr in range(FULL):
                        nc.tensor.matmul(ps[0:C, 0:4 * W], w2T[:, gr, :], acc[:, par, gr, q * 4 * W:(q + 1) * 4 * W],
                                         start=(gr == 0), stop=False)
                    u = 64 * (q // 2)
                    last = nc.tensor.matmul(ps[0:C, 0:4 * W], w2T[u:u + 64, FULL, :],
                                            acc[u:u + 64, par, FULL, (q % 2) * 4 * W:(q % 2 + 1) * 4 * W],
                                            start=False, stop=True)
                last.then_inc(misc_ready, 1)

            def pair(p):
                p %= PAIRS
                return p // PPC, (p % PPC) * 128

            def scores(b, P, p):
                c, o = pair(p)
                if o == 0:
                    if due(count := CHUNKS * b + p // PPC + 1):
                        pe.wait_ge(xn_ready, count)
                if due(count := P):
                    pe.wait_ge(idx_ready, count)
                S = pscore[:, 0:NODES]
                for w in range(2):
                    cols = xn[0:C + 1, c, o + 64 * w:o + 64 * w + 64]
                    Sw = S[64 * w:64 * w + 64, :]
                    nc.tensor.matmul(Sw, cols[0:C, :], cols[0:C, :], start=True, stop=False)
                    nc.tensor.matmul(Sw, onerow, cols[C:C + 1, :], start=False, stop=False)
                    last = nc.tensor.matmul(Sw, Imask, negI, start=False, stop=True)
                last.then_inc(score_ready, 1)

            def feature_transpose(P, p):
                if due(count := P + 1):
                    pe.wait_ge(feat_ready, count)
                if due(count := P - 1):
                    pe.wait_ge(self_gelu, count)
                nc.tensor.matmul(pself[0:32, 256:320], feat[:, p % 2].rearrange("p f n -> p (f n)"), I2,
                                 start=True, stop=True).then_inc(featT_ready, 1)

            def expand(P, p):
                if due(count := P + 1):
                    pe.wait_ge(featT_evac, count)
                if due(count := P):
                    pe.wait_ge(onehot_ready, count)
                for k in range(KN):
                    last = nc.tensor.matmul(pone[:, k, :], LK[:, k, :], featT[:, p % 2, :], start=True, stop=True)
                last.then_inc(onehot_in, 1)

            def values(P, p):
                c, o = pair(p)
                if due(count := P):
                    pe.wait_ge(vu_evac, count)
                nc.tensor.matmul(pvu[:, 0:O], y[:, c, o:o + 128], wVU[:, 0, :], start=True, stop=True)
                for w in range(2):
                    last = nc.tensor.matmul(pvu[64 * (1 - w):64 * (1 - w) + 64, O:2 * O],
                                            y[:, c, o + 64 * w:o + 64 * w + 64], wVU[:, 1, :], start=True, stop=True)
                last.then_inc(vu_ready, 1)

            def gather(P, p, part):
                n = 3 * P + part
                if due(count := n - 1):
                    pe.wait_ge(gelu_done, count)
                ps = pg[(3 * p + part) % 2]
                r = p % 2
                cols = [MV[:, r, w, 0:KN, :].rearrange("p k n -> p (k n)") for w in range(2)]
                if part < 2:
                    last = nc.tensor.matmul(ps[:, :], VU[:, r, part, 0:ONE128], cols[part], start=True, stop=True)
                else:
                    for w in range(2):
                        last = nc.tensor.matmul(ps[64 * w:64 * w + 64, :], VU[:, r, w, ONE128:O], cols[w],
                                                start=True, stop=True)
                last.then_inc(gather_ready, 1)

            def gather_self(P, p):
                r = p % 2
                for w in range(2):
                    nc.tensor.matmul(pself[:, 64 * w:64 * w + 64], VU[:, r, w, 0:ONE128], MV[:, r, w, KN, :],
                                     start=True, stop=True)
                for w in range(2):
                    last = nc.tensor.matmul(pself[64 * w:64 * w + 64, 128:192], VU[:, r, w, ONE128:O],
                                            MV[:, r, w, KN, :], start=True, stop=True)
                last.then_inc(self_ready, 1)

            pe.wait_ge(consts_ready, 1)

            def image(b, p0, p1):
                for p in range(p0, p1):
                    P = PAIRS * b + p
                    jobs = misc_jobs(b, p)
                    early = len(jobs) // 2
                    if valid(P + 1, NPAIRS):
                        feature_transpose(P + 1, p + 1)
                    if valid(P, NPAIRS):
                        if due(count := P + 1):
                            pe.wait_ge(onehot_ready, count)
                        if due(count := P + 1):
                            pe.wait_ge(vu_evac, count)
                        gather(P, p, 0)
                    if valid(P + 2, NPAIRS):
                        scores(b, P + 2, p + 2)
                    if valid(P + 1, NPAIRS):
                        expand(P + 1, p + 1)
                    if valid(P, NPAIRS):
                        gather(P, p, 1)
                    if valid(P + 1, NPAIRS):
                        values(P + 1, p + 1)
                    for k in range(early):
                        shared_job(b, p, k, jobs[k])
                    if valid(P, NPAIRS):
                        gather(P, p, 2)
                        gather_self(P, p)
                    for k in range(early, len(jobs)):
                        shared_job(b, p, k, jobs[k])

            image_loop(pe, image, TAIL)

        @block.scalar
        def _(act):
            def shared_evac(b, p, k, job):
                n = jobs_before(b) + jobs_in(b if isinstance(b, int) else 1, p) + k
                ps = pmisc[bank_of(b, p, k)]
                kind = job[0]
                act.wait_ge(misc_ready, n + 1)
                if kind == "fc1":
                    bi, c = job[1:]
                    if due(count := PAIRS * (bi - 1) + PPC * (c + 1)):
                        act.wait_ge(vu_ready, count)
                    if due(count := CHUNKS * (bi - 1) + c + 1):
                        act.wait_ge(xn_ready, count)
                    src = ps[0:C, :].rearrange("p (row win col) -> p row win col", row=WS, win=WS)
                    dst = y[0:C, c, :].rearrange("p (win row col) -> p row win col", win=WS, row=WS)
                    nc.scalar.activation(dst, src, ACT.Identity, bias=l0sc[:, 0:1],
                                         scale=col97(V97 + 1)).then_inc(misc_evac, 1)
                    act.wait_ge(misc_evac, n + 1)
                    nc.scalar.activation(ysq[:, c % 2, :], y[0:C, c, :], ACT.Square).then_inc(ysq_ready, 1)
                elif kind == "ssq":
                    bi, c = job[1:]
                    if c % 4 == 0:
                        if due(count := 2 * bi + c // 4):
                            act.wait_ge(inv_ready, count)
                    nc.scalar.activation(ssq[:, (c % 4) * PPC:(c % 4 + 1) * PPC], ps[:, 0:PPC],
                                         ACT.Copy).then_inc(misc_evac, 1)
                elif kind == "inv":
                    bi, c = job[1:]
                    if due(count := CHUNKS * bi + c - 1):
                        act.wait_ge(xn_ready, count)
                    nc.scalar.activation(invb[:, c % 2, :], ps[0:C + 1, :], ACT.Copy).then_inc(misc_evac, 1)
                elif kind == "fc2":
                    bc, c = job[1:]
                    if due(count := CHUNKS * (bc - 1) + c + 1):
                        act.wait_ge(out_added, count)
                    src = ps[0:C, :].rearrange("p (win row col) -> p win row col", win=WS, row=WS)
                    dst = x1[:, c * WS:(c + 1) * WS, :].rearrange("p row (win col) -> p win row col", win=WS)
                    nc.scalar.activation(dst, src, ACT.Identity, bias=l0sc[:, 1:2],
                                         scale=col97(V97 + 4)).then_inc(misc_evac, 1)
                elif kind == "w1":
                    s, gr, m = job[1:]
                    t = (p // SLOTS - 2) % STRIPS
                    if m == 0:
                        if due(count := tap_number(s - 1, gr, TAPS - 1)):
                            act.wait_ge(tap_done, count)
                    sc, sh = sc1[:, gr:gr + 1], sh1[:, gr:gr + 1]
                    if gr < FULL:
                        r0, r1 = 6 * m, 6 * m + 6
                        if t == 0 and m == 0:
                            r0 = 1
                            nc.scalar.activation(hpad[:, gr, 0, 1:W + 1], zrow[:, :], ACT.Copy)
                        if t == STRIPS - 1 and m == 2:
                            r1 -= 1
                            nc.scalar.activation(hpad[:, gr, STRIP + 1, 1:W + 1], zrow[:, :], ACT.Copy)
                        o = (r0 - 6 * m) * W
                        nc.scalar.activation(hpad[:, gr, r0:r1, 1:W + 1],
                                             ps[:, o:o + (r1 - r0) * W].rearrange("p (row col) -> p row col", col=W),
                                             ACT.Relu, bias=sh, scale=sc).then_inc(misc_evac, 1)
                    else:
                        edge = 0 if (t == 0 and m == 0) else 1 if (t == STRIPS - 1 and m == 1) else None
                        if edge is None:
                            nc.scalar.activation(hpad[:, gr, 5 * m:5 * m + 5, 1:W + 1],
                                                 ps[:, 0:5 * W].rearrange("p (row col) -> p row col", col=W),
                                                 ACT.Relu, bias=sh, scale=sc).then_inc(misc_evac, 1)
                        else:
                            zr = 9 * edge
                            h = 64 * edge
                            nc.scalar.activation(hpad[h:h + 64, gr, zr, 1:W + 1], zrow[h:h + 64, :], ACT.Copy)
                            for u in range(2):
                                r0, r1 = 5 * m, 5 * m + 5
                                if u == edge:
                                    r0, r1 = (1, 5) if edge == 0 else (5, 9)
                                o = (r0 - 5 * m) * W
                                h = 64 * u
                                last = nc.scalar.activation(
                                    hpad[h:h + 64, gr, r0:r1, 1:W + 1],
                                    ps[h:h + 64, o:o + (r1 - r0) * W].rearrange("p (row col) -> p row col", col=W),
                                    ACT.Relu, bias=sh[h:h + 64, :], scale=sc[h:h + 64, :])
                            last.then_inc(misc_evac, 1)
                else:
                    s, q = job[1:]
                    cc = q // 2
                    if q % 2 == 0:
                        if due(count := 16 * s):
                            act.wait_ge(store_done[cc], count)
                    nc.scalar.activation(res[:, cc, (q % 2) * 4 * W:(q % 2 + 1) * 4 * W], ps[0:C, 0:4 * W],
                                         ACT.Identity, bias=sc2[:, 1:2], scale=sc2[:, 0:1]).then_inc(misc_evac, 1)

            def featT_copy(P, p):
                act.wait_ge(featT_ready, P + 1)
                if due(count := P - 1):
                    act.wait_ge(onehot_in, count)
                nc.scalar.activation(featT[:, p % 2, :], pself[0:32, 256:320], ACT.Copy).then_inc(featT_evac, 1)

            def onehot(P, p):
                act.wait_ge(onehot_in, P + 1)
                if due(count := P - 1):
                    act.wait_ge(self_ready, count)
                for w in range(2):
                    h = 64 * w
                    last = nc.scalar.activation(MV[h:h + 64, p % 2, w, 0:KN, :], pone[h:h + 64, :, :], ACT.Relu,
                                                bias=nbias[h:h + 64, :], scale=1.0)
                last.then_inc(onehot_ready, 1)

            def vu_copy(P, p):
                act.wait_ge(vu_ready, P + 1)
                r = p % 2
                nc.scalar.activation(VU[0:64, r, 0, :], pvu[0:64, 0:O], ACT.Copy)
                nc.scalar.activation(VU[64:128, r, 0, :], pvu[64:128, O:2 * O], ACT.Copy)
                nc.scalar.activation(VU[0:64, r, 1, :], pvu[0:64, O:2 * O], ACT.Copy)
                nc.scalar.activation(VU[64:128, r, 1, :], pvu[64:128, 0:O], ACT.Copy).then_inc(vu_evac, 1)

            def gelu(P, p, part):
                act.wait_ge(gather_ready, 3 * P + part + 1)
                if part == 0:
                    if due(count := P - 1):
                        act.wait_ge(hid_ready, count)
                nc.scalar.activation(g[:, p % 2, part, 0:KN, :],
                                     pg[(3 * p + part) % 2][:, :].rearrange("p (k n) -> p k n", k=KN),
                                     ACT.Gelu).then_inc(gelu_done, 1)

            def gelu_self(P, p):
                act.wait_ge(self_ready, P + 1)
                nc.scalar.activation(g[:, p % 2, :, KN, :],
                                     pself[:, 0:192].rearrange("p (c n) -> p c n", c=3),
                                     ACT.Gelu).then_inc(self_gelu, 1)

            def relu2(b, p, s, par, groups):
                for gr in groups:
                    if due(count := tap_number(s, gr, TAPS - 1)):
                        act.wait_ge(tap_done, count)
                    n = STRIP * W if gr < FULL else STRIP * W // 2
                    nc.scalar.activation(acc[:, par, gr, 0:n], acc[:, par, gr, 0:n], ACT.Relu,
                                         bias=shd[:, gr:gr + 1], scale=scd[:, gr:gr + 1]).then_inc(relu_done, 1)

            act.wait_ge(bn_sqrt_in, 3)
            nc.scalar.activation(bn[:, 0:2, :], bn[:, 0:2, :], ACT.Sqrt).then_inc(bn_sqrt_out, 1)
            nc.scalar.activation(tmp2[:, 0:1], tmp2[:, 0:1], ACT.Sqrt).then_inc(bn_sqrt_out, 1)
            act.wait_ge(consts_ready, 1)

            def image(b, p0, p1):
                for p in range(p0, p1):
                    t, i = p // SLOTS, p % SLOTS
                    P = PAIRS * b + p
                    jobs = misc_jobs(b, p)
                    early = len(jobs) // 2
                    if valid(P + 1, NPAIRS):
                        featT_copy(P + 1, p + 1)
                    if valid(P, NPAIRS):
                        gelu(P, p, 0)
                    if valid(P + 1, NPAIRS):
                        onehot(P + 1, p + 1)
                    if valid(P, NPAIRS):
                        gelu(P, p, 1)
                    if valid(P + 1, NPAIRS):
                        vu_copy(P + 1, p + 1)
                    for k in range(early):
                        shared_evac(b, p, k, jobs[k])
                    if valid(P, NPAIRS):
                        gelu(P, p, 2)
                        gelu_self(P, p)
                    for k in range(early, len(jobs)):
                        shared_evac(b, p, k, jobs[k])
                    s = STRIPS * b + t - 2
                    if i == 5 and valid(s, NSTRIPS):
                        relu2(b, p, s, t % 2, (0, 1))
                    if i == 2 and valid(s - 1, NSTRIPS):
                        relu2(b, p, s - 1, (t - 1) % 2, (2, 3, 4))

            image_loop(act, image, TAIL)

        @block.vector
        def _(dve):
            steps = [0]

            def step(ins):
                steps[0] += 1
                ins.then_inc(dve_setup, 1)
                dve.wait_ge(dve_setup, steps[0])

            dve.wait_ge(param_load, 96)
            nc.vector.memset(hpad[:, :, :, :], 0.0)
            nc.vector.memset(zrow[:, :], 0.0)
            nc.vector.memset(expo[:, :], -0.5)
            nc.vector.memset(ones[:, :], 1.0)
            nc.vector.memset(onesq[:, :, :], 1.0)
            nc.vector.memset(y[C:C + 1, :, :], 1.0)
            step(nc.vector.tensor_copy(c16[:, :], c16f[:, :]))
            for r in range(2):
                for w in range(2):
                    v, u = 64 * w, 64 * (1 - w)
                    nc.vector.tensor_copy(MV[v:v + 64, r, w, KN, :], eye[v:v + 64, :])
                    step(nc.vector.tensor_copy(MV[u:u + 64, r, w, :, :],
                                               eye[u:u + 64, :].unsqueeze(1).to_broadcast([64, KN + 1, NODES])))
            es = r97[:, 0:O]
            step(nc.vector.tensor_tensor(wVU[:, 1, :], r97[:, O:2 * O], r97[:, 2 * O:3 * O], ALU.subtract))
            step(nc.vector.tensor_tensor(wVU[:, 1, :], wVU[:, 1, :], es, ALU.mult))
            step(nc.vector.tensor_tensor(wVU[:, 0, :], r97[:, 2 * O:3 * O], es, ALU.mult))
            step(nc.vector.tensor_tensor(wVU[C:C + 1, 1, :], wVU[C:C + 1, 1, :],
                                         w97[C:C + 1, 0:O], ALU.add))
            for k, v in ((0, V97), (1, V97 + 3)):
                step(nc.vector.tensor_tensor(l0sc[:, k:k + 1], col97(v), col97(v + 1), ALU.mult))
                step(nc.vector.tensor_tensor(l0sc[:, k:k + 1], l0sc[:, k:k + 1], col97(v + 2), ALU.add))
            EPS = 1e-5
            nc.vector.tensor_scalar(bn[:, 0, :], bnp[:, 3, :], EPS, None, ALU.add).then_inc(bn_sqrt_in, 1)
            nc.vector.tensor_scalar(bn[:, 1, :], bnp[:, 7, :], EPS, None, ALU.add).then_inc(bn_sqrt_in, 1)
            nc.vector.tensor_scalar(tmp2[:, 0:1], col97(V97 + 9), EPS, None, ALU.add).then_inc(bn_sqrt_in, 1)
            dve.wait_ge(bn_sqrt_out, 2)
            step(nc.vector.reciprocal(bn[:, 0:2, :], bn[:, 0:2, :]))
            step(nc.vector.reciprocal(tmp2[:, 0:1], tmp2[:, 0:1]))
            for k, (sc, sh) in enumerate(((sc1, sh1), (scd, shd))):
                step(nc.vector.tensor_tensor(sc[:, :], bnp[:, 4 * k, :], bn[:, k, :], ALU.mult))
                step(nc.vector.tensor_tensor(sh[:, :], bnp[:, 4 * k + 2, :], sc[:, :], ALU.mult))
                step(nc.vector.tensor_tensor(sh[:, :], bnp[:, 4 * k + 1, :], sh[:, :], ALU.subtract))
            step(nc.vector.tensor_tensor(sc2[:, 0:1], col97(V97 + 6), tmp2[:, 0:1], ALU.mult))
            step(nc.vector.tensor_tensor(sc2[:, 1:2], col97(V97 + 8), sc2[:, 0:1], ALU.mult))
            nc.vector.tensor_tensor(sc2[:, 1:2], col97(V97 + 7), sc2[:, 1:2], ALU.subtract).then_inc(consts_ready, 1)

            def neighbours(P, p):
                r = p % 2
                if due(count := P + 1):
                    dve.wait_ge(score_ready, count)
                dve.sem_inc(dve_passed, 1)
                nc.vector.max(top8[:, r, :], pscore[:, 0:NODES]).then_inc(top8_ready, 1)
                if due(count := P + 1):
                    dve.wait_ge(top8_ready, count)
                dve.sem_inc(dve_passed, 1)
                nc.vector.max_index(idx[:, r, :], top8[:, r, :], pscore[:, 0:NODES]).then_inc(idx_ready, 1)

            def features(P, p):
                r = p % 2
                if due(count := P + 1):
                    dve.wait_ge(idx_ready, count)
                if due(count := P - 1):
                    dve.wait_ge(featT_ready, count)
                fa = feat[:, r, 0, :].rearrange("p (win k) -> p win k", win=2)
                fb = feat[:, r, 1, :].rearrange("p (win k) -> p win k", win=2)
                nc.vector.scalar_tensor_tensor(out=fa, in0=idx[:, r, :].unsqueeze(1).to_broadcast([128, 2, KN]),
                                               scalar=-32.0, in1=maskw, op0=ALU.add, op1=ALU.mult).then_inc(a_ready, 1)
                if due(count := P + 1):
                    dve.wait_ge(a_ready, count)
                nc.vector.scalar_tensor_tensor(out=fb, in0=fa, scalar=-1.0, in1=fa, op0=ALU.mult,
                                               op1=ALU.mult).then_inc(feat_ready, 1)

            def diagonals(bi, c):
                if due(count := 2 * bi + c // 4 + 1):
                    dve.wait_ge(inv_ready, count)
                if due(count := CHUNKS * bi + c - 1):
                    dve.wait_ge(xn_ready, count)
                r = inv[:, (c % 4) * PPC:(c % 4 + 1) * PPC]
                nc.vector.tensor_tensor(diag[:, c % 2, :, :], eye128[:, :].unsqueeze(1).to_broadcast([128, PPC, 128]),
                                        r.unsqueeze(2).to_broadcast([128, PPC, 128]), ALU.mult).then_inc(diag_ready, 1)

            def normalise(b, p, bi, c):
                fb, fp = when(b, p, 1)
                if due(count := job_at(fb, fp, "inv", c)):
                    dve.wait_ge(misc_evac, count)
                if due(count := PAIRS * (bi - 1) + PPC * (c + 1)):
                    dve.wait_ge(score_ready, count)
                nc.vector.tensor_tensor(xn[:, c, :], y[:, c, :], invb[:, c % 2, :], ALU.mult).then_inc(xn_ready, 1)

            def maxima(P, p):
                c, j, r = (p % PAIRS) // PPC, p % PPC, p % 2
                if due(count := P + 1):
                    dve.wait_ge(self_gelu, count)
                nc.vector.tensor_reduce(hid[:, c % 2, j, :, :], g[:, r].rearrange("p c k n -> p c n k"),
                                        op=ALU.max, axis=AX.X).then_inc(hid_ready, 1)

            def tap(s, sp_, gr, k):
                dy, dx = k // 3, k % 3
                n = STRIP if gr < FULL else STRIP // 2
                src = hpad[:, gr, dy:dy + n, dx:dx + W]
                dst = acc[:, sp_, gr, 0:n * W].rearrange("p (row col) -> p row col", col=W)
                wk = wd[:, gr, k:k + 1]
                if k == 0:
                    ins = nc.vector.tensor_scalar(dst, src, wk, None, ALU.mult)
                else:
                    if due(count := tap_number(s, gr, k - 1)):
                        dve.wait_ge(tap_done, count)
                    ins = nc.vector.scalar_tensor_tensor(out=dst, in0=src, scalar=wk, in1=dst, op0=ALU.mult,
                                                         op1=ALU.add)
                ins.then_inc(tap_done, 1)

            def add_residual(b, p, c, bc):
                fb, fp = when(b, p, 1)
                if due(count := job_at(fb, fp, "fc2", c)):
                    dve.wait_ge(misc_evac, count)
                if due(count := 16 * (2 * bc + c // 4 + 1)):
                    dve.wait_ge(xres_load[c % 4], count)
                part = x1[:, c * WS:(c + 1) * WS, :].rearrange("p row col -> p (row col)")
                nc.vector.tensor_tensor(part, part, xres[:, c % 4, :], ALU.add).then_inc(x1_ready, 1)

            def add_output(b, p, cc, c):
                fb, fp = when(b, p, 1)
                if due(count := job_at(fb, fp, "w2", 2 * cc + 1)):
                    dve.wait_ge(misc_evac, count)
                part = x1[:, c * WS:(c + 1) * WS, :].rearrange("p row col -> p (row col)")
                nc.vector.tensor_tensor(res[:, cc, :], res[:, cc, :], part, ALU.add).then_inc(out_added, 1)

            def image(b, p0, p1):
                for p in range(p0, p1):
                    t, i = p // SLOTS, p % SLOTS
                    P = PAIRS * b + p
                    s = STRIPS * b + t - 2
                    mine, previous = taps_of(i)
                    taps = [(s, t % 2, gr, k) for gr, k in mine if valid(s, NSTRIPS)]
                    taps += [(s - 1, (t - 1) % 2, gr, k) for gr, k in previous if valid(s - 1, NSTRIPS)]
                    new = valid(P + 2, NPAIRS)
                    if taps and taps[0][2:] in ((0, 0), (2, 0)):
                        gr = 1 if taps[0][2] == 0 else FULL
                        if due(count := job_at(b, p - i + gr, "w1", 2 if gr < FULL else 1)):
                            dve.wait_ge(misc_evac, count)
                    for a in taps[:2]:
                        tap(*a)
                    h = 1 if p < 16 else 0
                    bi = b if h else b + 1
                    if 10 <= p % 16 <= 13 and valid(bi, B):
                        normalise(b, p, bi, 4 * h + p % 16 - 10)
                    if 8 <= p % 16 <= 11 and valid(bi, B):
                        diagonals(bi, 4 * h + p % 16 - 8)
                    if p % 4 == 2:
                        bc, c = (b, (p - 6) // 4) if p >= 6 else (b - 1, CHUNKS - 1)
                        if valid(bc, B):
                            add_residual(b, p, c, bc)
                    if new:
                        neighbours(P + 2, p + 2)
                    for a in taps[2:3]:
                        tap(*a)
                    if new:
                        features(P + 2, p + 2)
                    for a in taps[3:]:
                        tap(*a)
                    if valid(P - 1, NPAIRS):
                        maxima(P - 1, p - 1)
                    if i == 6 and valid(s - 1, NSTRIPS):
                        add_output(b, p, 0, 2 * ((t - 3) % STRIPS))
                    if i == 0 and valid(s - 2, NSTRIPS):
                        add_output(b, p, 1, 2 * ((t - 4) % STRIPS) + 1)

            image_loop(dve, image, TAIL)


TAIL = 3 * SLOTS + 1
P97 = C + HID + 12
P128 = 8 * C + 45 + 40
CF = 81 + NODES
C16 = 256 + KN * 128


def kernel(**inputs):
    import numpy as np
    import concourse.bacc as bacc
    from concourse.bass_utils import run_bass_kernel_spmd as run

    f = {k: np.ascontiguousarray(v) for k, v in inputs.items()}

    def l0(n):
        return f["L0_conv_" + n]

    def l1(n):
        return f["L1_conv_" + n]

    def grouped(v):
        v = v.reshape(HID, -1)
        full = v[:FULL * 128].reshape(FULL, 128, -1).transpose(1, 0, 2)
        half = np.concatenate([v[FULL * 128:]] * 2, 0)[:, None, :]
        return np.concatenate([full, half], 1)

    p97 = np.zeros((C + 1, P97), np.float32)
    p97[:C, :C] = l0("fc1_w").T
    p97[:C, C:C + HID] = l1("w1").T
    p97[C, :O] = l0("et")
    names = [l0("fc1_b"), l0("fc1_s"), l0("fc1_t"), l0("fc2_b"), l0("fc2_s"), l0("fc2_t"),
             l1("g2"), l1("b2"), l1("m2"), l1("v2")]
    for k, v in enumerate(names):
        p97[:C, C + HID + k] = v
    fc2T = l0("fc2_w").T
    zeros = np.zeros((O - ONE128, C), np.float32)
    p128 = np.concatenate([
        fc2T[:ONE128], np.concatenate([fc2T[ONE128:], zeros], 0), np.concatenate([zeros, fc2T[ONE128:]], 0),
        grouped(l1("w2").T).reshape(128, -1), grouped(l1("wd")).reshape(128, -1),
    ] + [grouped(l1(n)).reshape(128, 5) for n in ("g1", "b1", "m1", "v1", "gd", "bd", "md", "vd")], 1)
    ewT = l0("ew").T
    rows97 = np.zeros((C + 1, 3 * O), np.float32)
    rows97[:, :O] = l0("es")
    rows97[:C, O:2 * O] = ewT[:C]
    rows97[C, O:2 * O] = l0("eb")
    rows97[:C, 2 * O:] = ewT[C:]
    j = np.arange(128) % NODES - 32
    eye = np.eye(NODES, dtype=np.float32)
    cst = np.zeros((128, CF), np.float32)
    cst[:, 0] = 1 - j * j
    cst[:64, 1:9] = 1
    cst[64:, 9:17] = 1
    cst[:, 17:81] = 1
    cst[:, 81:] = np.concatenate([eye, eye], 0)
    c16 = np.zeros((128, C16), np.float32)
    c16[:, 0:64] = np.concatenate([eye, eye], 0)
    c16[:64, 64:192] = np.concatenate([eye, eye], 1)
    c16[:64, 192:256] = -8 * eye
    lk = np.zeros((2, 2, KN, KN, 2, NODES), np.float32)
    for w in range(2):
        for k in range(KN):
            lk[0, w, k, k, w] = 2 * j[:NODES]
            lk[1, w, k, k, w] = 1
    c16[:32, 256:] = lk.reshape(32, -1)

    arrays = {"x": f["x"], "p97": p97, "p128": np.ascontiguousarray(p128), "rows97": rows97, "consts": cst,
              "consts128": np.eye(128, dtype=np.float32), "consts16": c16}
    nc = bacc.Bacc("TRN2", target_bir_lowering=False, num_devices=1)
    args = [nc.dram_tensor(f"in_{n}_dram", a.shape, mybir.dt.from_np(a.dtype), kind="ExternalInput").ap()
            for n, a in arrays.items()]
    out = nc.dram_tensor("out_0_dram", f["x"].shape, mybir.dt.float32, kind="ExternalOutput").ap()
    build(nc, *args, out)
    r = run(nc, [{f"in_{n}_dram": a for n, a in arrays.items()}], core_ids=[0])
    return r.results[0]["out_0_dram"]
```

```python
import concourse.bass as bass
from concourse import mybir
from contextlib import ExitStack

B, C, H, W = 16, 96, 64, 64
WS = 8
NODES = WS * WS
O = 2 * C
KN = 8
HID = 576
FULL, HALF = HID // 128, HID % 128
PAIRS = (H // WS) * (W // WS) // 2
CHUNKS = H // WS
PPC = PAIRS // CHUNKS
CW = WS * W
STRIP = 16
STRIPS = H // STRIP
SLOTS = PAIRS // STRIPS
TAPS = 9
PADW = W + 2
ONE128 = 128
NPAIRS, NSTRIPS = B * PAIRS, B * STRIPS


def valid(v, n):
    return not isinstance(v, int) or 0 <= v < n


FC1_AT = {1: 0, 2: 1, 4: 2, 5: 3}
SSQ_AT = {2: 0, 3: 1, 5: 2, 6: 3}
NORMS_AT = 7
DIAG_AT = {8: 0, 10: 1, 11: 2, 12: 3}
INV_AT = {9: 0, 11: 1, 12: 2, 13: 3}
XN_AT = {10: 0, 12: 1, 13: 2, 14: 3}
W1_AT = {-2: [(0, 0), (0, 1)], -1: [(0, 2)], 0: [(1, 0), (1, 1)], 1: [(1, 2), (2, 0)],
         2: [(2, 1), (2, 2), (3, 0)], 3: [(3, 1), (3, 2), (4, 0)], 4: [(4, 1)]}
TAP0_AT = {5: [4]}
TAP0_LATE = {0: [0], 1: [1], 2: [2], 4: [3]}
RELU2_AT = {6: [0], 7: [1], 10: [2], 11: [3, 4]}
W2_AT = {12: 0, 14: 1, 15: 2, 16: 3}
TAP_COUNTS = [5, 4, 4, 6, 4, 5, 6, 6]
ORDER = ('ssq', 'fc1', 'inv', 'fc2', 'w1', 'w2')
STORE_AT = {o + 1: q for o, q in W2_AT.items() if q % 2 == 1}
FIRST = [(g, k) for k in range(1, TAPS) for g in (0, 1)]
SECOND = [(g, k) for k in range(1, TAPS) for g in (2, 3, 4)]
TAP_AT = {2 + n: (FIRST + SECOND)[sum(TAP_COUNTS[:n]):sum(TAP_COUNTS[:n + 1])]
          for n in range(SLOTS)}


def w1_slot(gr, m):
    return next(o for o, parts in W1_AT.items() if (gr, m) in parts)


def due_in(table, b, p):
    found = []
    for o in sorted(table, reverse=True):
        if (p - o) % SLOTS == 0:
            k = (p - o) // SLOTS - 2
            if valid(STRIPS * b + k, NSTRIPS):
                found.append((o, k % STRIPS, STRIPS * b + k, table[o]))
    return found


def misc_jobs(b, p):
    jobs = []
    half = p // 16
    bi = b + half
    c0 = 4 if half == 0 else 0
    q = p % 16
    if valid(bi, B):
        if q in FC1_AT:
            jobs.append(("fc1", bi, c0 + FC1_AT[q]))
        if q in SSQ_AT:
            jobs.append(("ssq", bi, c0 + SSQ_AT[q]))
        if q in INV_AT:
            jobs.append(("inv", bi, c0 + INV_AT[q]))
    if p % 4 == 1:
        bc, c = (b, (p - 5) // 4) if p >= 5 else (b - 1, CHUNKS - 1)
        if valid(bc, B):
            jobs.append(("fc2", bc, c))
    for _, t, s, fours in due_in(W2_AT, b, p):
        jobs.append(("w2", t, s, fours))
    for _, t, s, parts in due_in(W1_AT, b, p):
        jobs += [("w1", t, s, part) for part in parts]
    jobs.sort(key=lambda job: ORDER.index(job[0]))
    return jobs


PART_STARTS = (0.25, 0.5, 0.75)


def part_of(jobs, part):
    return [k for k in range(len(jobs)) if sum(k >= f * len(jobs) for f in PART_STARTS) == part]


def jobs_in(b, upto=PAIRS):
    return sum(len(misc_jobs(b, p)) for p in range(16 if b < 0 else 0, upto))


PER_IMAGE = jobs_in(1)
BEFORE = {-1: 0, 0: jobs_in(-1)}
BEFORE[1] = BEFORE[0] + jobs_in(0)
for _b in range(2, B):
    BEFORE[_b] = BEFORE[1] + (_b - 1) * PER_IMAGE
BEFORE[B] = BEFORE[B - 1] + jobs_in(B - 1)


def jobs_before(b):
    return BEFORE[b] if isinstance(b, int) else BEFORE[1] + (b - 1) * PER_IMAGE


def job_at(b, p, kind, which):
    n = 0
    for pp in range(16 if isinstance(b, int) and b < 0 else 0, PAIRS):
        for j in misc_jobs(b, pp):
            n += 1
            if pp == p and j[0] == kind and j[-1] == which:
                return jobs_before(b) + n
    raise AssertionError((b, p, kind, which))


def bank_of(b, p, k):
    if not isinstance(b, int):
        b = 1
    return (jobs_before(b) + jobs_in(b, p) + k) % 2


def when(b, p, ago):
    p -= ago
    return (b, p) if p >= 0 else (b - 1, p + PAIRS)


def tap_number(s, g, k):
    k -= 1
    return s * 5 * (TAPS - 1) + (2 * k + g if g < 2 else 2 * (TAPS - 1) + 3 * k + g - 2) + 1


def due(count):
    return not isinstance(count, int) or count > 0


def build(nc, x, p97, p128, rows97, consts, consts128, consts16, out):
    f32, f16, u32 = mybir.dt.float32, mybir.dt.float16, mybir.dt.uint32
    ALU, ACT, AX = mybir.AluOpType, mybir.ActivationFunctionType, mybir.AxisListType
    ctx = ExitStack()
    with ctx:
        def sb(name, shape, dt=f32):
            return ctx.enter_context(nc.sbuf_tensor(name, shape, dt))

        def pb(name, shape):
            return ctx.enter_context(nc.psum_tensor(name, shape, f32))

        def sem(name):
            return ctx.enter_context(nc.semaphore(name))

        w97 = sb("w97", [C + 1, P97])
        w128 = sb("w128", [128, P128])
        cst = sb("cst", [128, CF])
        ones = sb("ones", [C, 1])
        onesq = sb("onesq", [128, 4 * PPC, C + 1])
        eye128 = sb("eye128", [128, 128])
        c16 = sb("c16", [128, C16], f16)
        wVU = sb("wVU", [C + 1, 2, O])
        l0sc = sb("l0sc", [C, 2])
        bn = sb("bn", [128, 3, 5])
        sc1, sh1 = sb("sc1", [128, 5]), sb("sh1", [128, 5])
        scd, shd = sb("scd", [128, 5]), sb("shd", [128, 5])
        sc2 = sb("sc2", [C, 2])
        tmp2 = sb("tmp2", [C, 2])
        zrow = sb("zrow", [128, W])
        expo = sb("expo", [128, 1])

        def col97(k):
            return w97[0:C, k:k + 1]

        fc1T = w97[0:C, 0:C]
        w1T = w97[0:C, C:C + HID]
        V97 = C + HID
        fc2T = w128[:, 0:3 * C].rearrange("p (k c) -> p k c", k=3)
        w2T = w128[:, 3 * C:8 * C].rearrange("p (g c) -> p g c", g=5)
        wd = w128[:, 8 * C:8 * C + 45].rearrange("p (g k) -> p g k", g=5)
        bnp = w128[:, 8 * C + 45:8 * C + 85].rearrange("p (n g) -> p n g", n=8)
        o_ = 8 * C + 85
        fc2s_row, g2_row, v2_row = (w128[:, o_ + k * C:o_ + (k + 1) * C] for k in range(3))
        nbias = cst[:, 0:1]
        maskw = cst[:, 1:17].rearrange("p (win k) -> p win k", win=2)
        onerow = cst[C:C + 1, 17:17 + NODES]
        eye = cst[:, 81:81 + NODES]
        I2 = c16[:, 0:NODES]
        Imask = c16[0:64, 64:128]
        negI = c16[0:64, 192:256]
        LK = c16[0:32, 256:256 + KN * 128].rearrange("p (k m) -> p k m", k=KN)

        xin = sb("xin", [C, 2, 4 * CW])
        xres = sb("xres", [C, 4, CW])
        y = sb("y", [C + 1, CHUNKS, CW])
        xn = sb("xn", [C + 1, CHUNKS, CW])
        ysq = sb("ysq", [C, 2, CW])
        ssq = sb("ssq", [128, 4 * PPC])
        clamped = sb("clamped", [128, 4 * PPC])
        inv = sb("inv", [128, 4 * PPC])
        sqn = sb("sqn", [128, 4 * PPC])
        diag = sb("diag", [128, 2, PPC, 128])
        invb = sb("invb", [C + 1, 2, CW])
        top8 = sb("top8", [128, 2, 8])
        idx = sb("idx", [128, 2, 8], u32)
        feat = sb("feat", [128, 2, 2, 2 * KN], f16)
        featT = sb("featT", [32, 2, NODES], f16)
        VU = sb("VU", [128, 2, 2, O])
        MV = sb("MV", [128, 2, 2, KN + 1, NODES])
        g = sb("g", [128, 2, 3, KN + 1, NODES])
        gflat = g[:, 0].rearrange("p c k n -> p (c k n)")
        c16f = gflat[:, 0:C16]
        r97 = g[0:C + 1, 1].rearrange("p c k n -> p (c k n)")[:, 0:3 * O]
        hid = sb("hid", [128, 2, PPC, 3, NODES])
        x1 = sb("x1", [C, H, W])
        hpad = sb("hpad", [128, 5, STRIP + 2, PADW])
        acc = sb("acc", [128, 2, 5, STRIP * W])
        res = sb("res", [C, 2, CW])

        pmisc = [pb(f"pmisc{k}", [128, 512]) for k in range(2)]
        pscore = pb("pscore", [128, 512])
        pself = pb("pself", [128, 512])
        pone = pb("pone", [128, KN, NODES])
        pvu = pb("pvu", [128, 512])
        pg = [pb(f"pg{k}", [128, 512]) for k in range(2)]

        w97_load, param_load, consts_ready, bn_sqrt_in, bn_sqrt_out = (sem(n) for n in (
            "w97_load", "param_load", "consts_ready", "bn_sqrt_in", "bn_sqrt_out"))
        dve_setup, act_setup = sem("dve_setup"), sem("act_setup")
        xin_load = [sem(f"xin_load{k}") for k in range(2)]
        xres_load = [sem(f"xres_load{k}") for k in range(4)]
        store_done = [sem(f"store_done{k}") for k in range(2)]
        misc_ready, misc_evac = sem("misc_ready"), sem("misc_evac")
        ysq_ready, pool_step, inv_ready, diag_ready, xn_ready = (sem(n) for n in (
            "ysq_ready", "pool_step", "inv_ready", "diag_ready", "xn_ready"))
        score_ready, top8_ready, idx_ready, a_ready, feat_ready = (sem(n) for n in (
            "score_ready", "top8_ready", "idx_ready", "a_ready", "feat_ready"))
        featT_ready, featT_evac, onehot_in, onehot_ready = (sem(n) for n in (
            "featT_ready", "featT_evac", "onehot_in", "onehot_ready"))
        vu_ready, vu_evac, gather_ready, self_ready, gelu_done, self_gelu = (sem(n) for n in (
            "vu_ready", "vu_evac", "gather_ready", "self_ready", "gelu_done", "self_gelu"))
        sp_passed, pool_passed, dve_passed = sem("sp_passed"), sem("pool_passed"), sem("dve_passed")
        hid_ready, tap0_done, tap_done, relu_done = (sem(n) for n in (
            "hid_ready", "tap0_done", "tap_done", "relu_done"))

        block = ctx.enter_context(nc.Block())

        def image_loop(eng, image, tail):
            image(-1, 16, PAIRS)
            image(0, 0, PAIRS)
            with eng.Fori(1, B - 1) as b:
                image(b, 0, PAIRS)
            image(B - 1, 0, PAIRS)
            image(B, 0, tail)

        @block.sync
        def _(sp):
            xv = x.rearrange("b c row col -> b c (row col)")
            ov = out.rearrange("b c row col -> b c (row col)")

            def load_half(b, h):
                sp.dma_start(xin[:, h, :], xv[b, :, h * 4 * CW:(h + 1) * 4 * CW]).then_inc(xin_load[h], 16)

            def load_res(b, c):
                sp.dma_start(xres[:, c % 4, :], xv[b, :, c * CW:(c + 1) * CW]).then_inc(xres_load[c % 4], 16)

            sp.dma_start(w97[:, :], p97).then_inc(w97_load, 16)
            load_half(0, 0)
            sp.dma_start(w128[:, :], p128).then_inc(param_load, 16)
            sp.dma_start(r97[:, :], rows97).then_inc(param_load, 16)
            sp.dma_start(cst[:, :], consts).then_inc(param_load, 16)
            sp.dma_start(eye128[:, :], consts128).then_inc(param_load, 16)
            sp.dma_start(c16f[:, :], consts16).then_inc(param_load, 16)
            load_half(0, 1)

            def image(b, p0, p1):
                for p in range(p0, p1):
                    if p in (1, 8) and valid(b, B) and valid(b + 1, B):
                        h = p // 8
                        if due(count := CHUNKS * b + 4 * h + 4):
                            sp.wait_ge(ysq_ready, count)
                        sp.sem_inc(sp_passed, 1)
                        load_half(b + 1, h)
                    if isinstance(b, int) and b == -1 and p >= 28:
                        load_res(0, p - 28)
                    if p % 4 == 2:
                        bc, c = (b, (p - 6) // 4) if p >= 6 else (b - 1, CHUNKS - 1)
                        bl, cl = (bc, c + 4) if c < 4 else (bc + 1, c - 4)
                        if valid(bc, B) and valid(bl, B):
                            fb, fp = when(b, p, 1)
                            sp.wait_ge(misc_evac, job_at(fb, fp, "fc2", c))
                            sp.sem_inc(sp_passed, 1)
                            load_res(bl, cl)
                    for o, t, s, q in due_in(STORE_AT, b, p):
                        fb, fp = when(b, p, 1)
                        sp.wait_ge(misc_evac, job_at(fb, fp, "w2", q))
                        sp.sem_inc(sp_passed, 1)
                        c = 2 * t + q // 2
                        bs = b if p - o >= 2 * SLOTS else b - 1
                        sp.dma_start(ov[bs, :, c * CW:(c + 1) * CW], res[:, q // 2, :]).then_inc(
                            store_done[q // 2], 16)

            image_loop(sp, image, TAIL)
            for k in range(2):
                sp.wait_ge(store_done[k], 16 * NSTRIPS)

        @block.gpsimd
        def _(pool):
            pool.wait_ge(consts_ready, 2)

            def inverse_norms(b, p, bi, h):
                n = 2 * bi + h
                fb, fp = when(b, p, 1)
                if due(count := job_at(fb, fp, "ssq", 4 * h + 3)):
                    pool.wait_ge(misc_evac, count)
                if due(count := 4 * n):
                    pool.wait_ge(diag_ready, count)
                pool.sem_inc(pool_passed, 1)
                nc.gpsimd.tensor_scalar(clamped[:, :], ssq[:, :], 1e-24, None, ALU.max).then_inc(pool_step, 1)
                pool.wait_ge(pool_step, 3 * n + 1)
                nc.gpsimd.tensor_tensor(inv[:, :], clamped[:, :], expo[:, 0:1].to_broadcast([128, 4 * PPC]),
                                        ALU.pow).then_inc(pool_step, 1)
                pool.wait_ge(pool_step, 3 * n + 2)
                nc.gpsimd.tensor_tensor(sqn[:, :], ssq[:, :], inv[:, :], ALU.mult).then_inc(pool_step, 1)
                pool.wait_ge(pool_step, 3 * n + 3)
                if due(count := 4 * n):
                    pool.wait_ge(xn_ready, count)
                pool.sem_inc(pool_passed, 1)
                nc.gpsimd.tensor_scalar(onesq[:, :, C], sqn[:, :], -0.5, None, ALU.mult).then_inc(inv_ready, 1)

            def image(b, p0, p1):
                for p in range(p0, p1):
                    if p % 16 == NORMS_AT:
                        h = 1 if p < 16 else 0
                        bi = b if h else b + 1
                        if valid(bi, B):
                            inverse_norms(b, p, bi, h)

            image_loop(pool, image, TAIL)

        @block.tensor
        def _(pe):
            def shared_job(b, p, k, job):
                n = jobs_before(b) + jobs_in(b if isinstance(b, int) else 1, p) + k
                if due(count := n - 1):
                    pe.wait_ge(misc_evac, count)
                ps = pmisc[bank_of(b, p, k)]
                kind = job[0]
                if kind == "fc1":
                    bi, c = job[1:]
                    if c % 4 == 0:
                        if due(count := 16 * (bi + 1)):
                            pe.wait_ge(xin_load[c // 4], count)
                    last = nc.tensor.matmul(ps[0:C, :], fc1T, xin[:, c // 4, (c % 4) * CW:(c % 4 + 1) * CW],
                                            start=True, stop=True)
                elif kind == "ssq":
                    bi, c = job[1:]
                    if due(count := CHUNKS * bi + c + 1):
                        pe.wait_ge(ysq_ready, count)
                    for j in range(PPC):
                        last = nc.tensor.matmul(ps[:, j:j + 1], ysq[:, c % 2, j * 128:(j + 1) * 128], ones[:, :],
                                                start=True, stop=True)
                elif kind == "inv":
                    bi, c = job[1:]
                    if due(count := CHUNKS * bi + c + 1):
                        pe.wait_ge(diag_ready, count)
                    for j in range(PPC):
                        last = nc.tensor.matmul(ps[0:C + 1, j * 128:(j + 1) * 128], onesq[:, (c % 4) * PPC + j, :],
                                                diag[:, c % 2, j, :], start=True, stop=True)
                elif kind == "fc2":
                    bc, c = job[1:]
                    if due(count := PAIRS * bc + PPC * (c + 1)):
                        pe.wait_ge(hid_ready, count)
                    hc = hid[:, c % 2]
                    pw = ps[0:C, :].rearrange("p (q win n) -> p q win n", q=PPC, win=2)
                    for w in range(2):
                        nc.tensor.matmul(pw[:, :, w, :], fc2T[:, 1 + w, :], hc[:, :, 2, :], start=(w == 0),
                                         stop=False)
                    nc.tensor.matmul(ps[0:C, :].rearrange("p (q n) -> p q n", q=PPC), fc2T[:, 0, :],
                                     hc[:, :, 0:2, :].rearrange("p q win n -> p q (win n)"), start=False, stop=False)
                    pe.wait_ge(xres_load[c % 4], 16 * (2 * bc + c // 4 + 1))
                    last = nc.tensor.matmul(ps[0:C, :].rearrange("p (win row col) -> p win row col", win=WS, row=WS),
                                            eye128[0:C, 0:C],
                                            xres[:, c % 4, :].rearrange("p (row win col) -> p win row col", row=WS,
                                                                        win=WS), start=False, stop=True)
                elif kind == "w1":
                    t, s, (gr, m) = job[1:]
                    if gr == 0 and m == 0:
                        c = min(2 * t + 2, CHUNKS - 1)
                        fb, fp = when(b, p, w1_slot(0, 0) + (3 if c % 2 == 0 else 7))
                        pe.wait_ge(misc_evac, job_at(fb, fp, "fc2", c))
                    top = STRIP * t - 1
                    if gr < FULL:
                        r0, r1 = 6 * m, 6 * m + 6
                        lo, hi = max(top + r0, 0), min(top + r1, H)
                        o = (lo - top - r0) * W
                        last = nc.tensor.matmul(ps[:, o:o + (hi - lo) * W], w1T[:, gr * 128:(gr + 1) * 128],
                                                x1[:, lo:hi, :], start=True, stop=True)
                    else:
                        for u in range(2):
                            first = top + 8 * u + 5 * m
                            lo, hi = max(first, 0), min(first + 5, H)
                            o = (lo - first) * W
                            last = nc.tensor.matmul(ps[64 * u:64 * u + 64, o:o + (hi - lo) * W],
                                                    w1T[:, FULL * 128:HID], x1[:, lo:hi, :], start=True, stop=True)
                else:
                    t, s, q = job[1:]
                    par = t % 2
                    if q == 0:
                        if due(count := 5 * (s + 1)):
                            pe.wait_ge(relu_done, count)
                    for gr in range(FULL):
                        nc.tensor.matmul(ps[0:C, 0:4 * W], w2T[:, gr, :], acc[:, par, gr, q * 4 * W:(q + 1) * 4 * W],
                                         start=(gr == 0), stop=False)
                    u = 64 * (q // 2)
                    nc.tensor.matmul(ps[0:C, 0:4 * W], w2T[u:u + 64, FULL, :],
                                     acc[u:u + 64, par, FULL, (q % 2) * 4 * W:(q % 2 + 1) * 4 * W],
                                     start=False, stop=False)
                    row = STRIP * t + 4 * q
                    last = nc.tensor.matmul(ps[0:C, 0:4 * W], eye128[0:C, 0:C], x1[:, row:row + 4, :],
                                            start=False, stop=True)
                last.then_inc(misc_ready, 1)

            def pair(p):
                p %= PAIRS
                return p // PPC, (p % PPC) * 128

            def scores(b, P, p):
                c, o = pair(p)
                if o == 0:
                    if due(count := CHUNKS * b + p // PPC + 1):
                        pe.wait_ge(xn_ready, count)
                if due(count := P):
                    pe.wait_ge(idx_ready, count)
                S = pscore[:, 0:NODES]
                for w in range(2):
                    cols = xn[0:C + 1, c, o + 64 * w:o + 64 * w + 64]
                    Sw = S[64 * w:64 * w + 64, :]
                    nc.tensor.matmul(Sw, cols[0:C, :], cols[0:C, :], start=True, stop=False)
                    nc.tensor.matmul(Sw, onerow, cols[C:C + 1, :], start=False, stop=False)
                    last = nc.tensor.matmul(Sw, Imask, negI, start=False, stop=True)
                last.then_inc(score_ready, 1)

            def feature_transpose(P, p):
                if due(count := P + 1):
                    pe.wait_ge(feat_ready, count)
                if due(count := P - 2):
                    pe.wait_ge(self_gelu, count)
                if due(count := P):
                    pe.wait_ge(featT_evac, count)
                nc.tensor.matmul(pself[0:32, 256:320], feat[:, p % 2].rearrange("p f n -> p (f n)"), I2,
                                 start=True, stop=True).then_inc(featT_ready, 1)

            def expand(P, p):
                if due(count := P + 1):
                    pe.wait_ge(featT_evac, count)
                if due(count := P):
                    pe.wait_ge(onehot_ready, count)
                for k in range(KN):
                    last = nc.tensor.matmul(pone[:, k, :], LK[:, k, :], featT[:, p % 2, :], start=True, stop=True)
                last.then_inc(onehot_in, 1)

            def values(P, p):
                c, o = pair(p)
                if due(count := P):
                    pe.wait_ge(vu_evac, count)
                for w in range(2):
                    nodes = y[:, c, o + NODES * w:o + NODES * (w + 1)]
                    for k in range(2):
                        h = 64 * (w ^ k)
                        last = nc.tensor.matmul(pvu[h:h + 64, O * w:O * (w + 1)], nodes, wVU[:, k, :], start=True,
                                                stop=True)
                last.then_inc(vu_ready, 1)

            def gather(P, p, part):
                n = 3 * P + part
                if due(count := n - 1):
                    pe.wait_ge(gelu_done, count)
                ps = pg[(3 * p + part) % 2]
                r = p % 2
                cols = [MV[:, r, w, 0:KN, :].rearrange("p k n -> p (k n)") for w in range(2)]
                if part < 2:
                    last = nc.tensor.matmul(ps[:, :], VU[:, r, part, 0:ONE128], cols[part], start=True, stop=True)
                else:
                    for w in range(2):
                        last = nc.tensor.matmul(ps[64 * w:64 * w + 64, :], VU[:, r, w, ONE128:O], cols[w],
                                                start=True, stop=True)
                last.then_inc(gather_ready, 1)

            def gather_self(P, p):
                r = p % 2
                pe.wait_ge(featT_evac, P + 3 if not isinstance(P, int) else min(P + 3, NPAIRS))
                for w in range(2):
                    nc.tensor.matmul(pself[:, 64 * w:64 * w + 64], VU[:, r, w, 0:ONE128], MV[:, r, w, KN, :],
                                     start=True, stop=True)
                for w in range(2):
                    last = nc.tensor.matmul(pself[64 * w:64 * w + 64, 128:192], VU[:, r, w, ONE128:O],
                                            MV[:, r, w, KN, :], start=True, stop=True)
                last.then_inc(self_ready, 1)

            pe.wait_ge(consts_ready, 1)

            def image(b, p0, p1):
                for p in range(p0, p1):
                    P = PAIRS * b + p
                    if isinstance(b, int) and b == -1 and p == 16 + NORMS_AT:
                        pe.wait_ge(consts_ready, 2)
                    jobs = misc_jobs(b, p)
                    if valid(P + 3, NPAIRS):
                        scores(b, P + 3, p + 3)
                    if valid(P, NPAIRS):
                        if due(count := P + 1):
                            pe.wait_ge(onehot_ready, count)
                        if due(count := P + 1):
                            pe.wait_ge(vu_evac, count)
                        gather(P, p, 0)
                    for k in part_of(jobs, 0):
                        shared_job(b, p, k, jobs[k])
                    if valid(P + 1, NPAIRS):
                        expand(P + 1, p + 1)
                    if valid(P + 2, NPAIRS):
                        feature_transpose(P + 2, p + 2)
                    if valid(P, NPAIRS):
                        gather(P, p, 1)
                    for k in part_of(jobs, 1):
                        shared_job(b, p, k, jobs[k])
                    if valid(P + 1, NPAIRS):
                        values(P + 1, p + 1)
                    if valid(P, NPAIRS):
                        gather(P, p, 2)
                    for k in part_of(jobs, 2):
                        shared_job(b, p, k, jobs[k])
                    if valid(P, NPAIRS):
                        gather_self(P, p)
                    for k in part_of(jobs, 3):
                        shared_job(b, p, k, jobs[k])

            image_loop(pe, image, TAIL)

        @block.scalar
        def _(act):
            def shared_evac(b, p, k, job):
                n = jobs_before(b) + jobs_in(b if isinstance(b, int) else 1, p) + k
                ps = pmisc[bank_of(b, p, k)]
                kind = job[0]
                act.wait_ge(misc_ready, n + 1)
                if kind == "fc1":
                    bi, c = job[1:]
                    if due(count := PAIRS * (bi - 1) + PPC * (c + 1)):
                        act.wait_ge(vu_ready, count)
                    if due(count := CHUNKS * (bi - 1) + c + 1):
                        act.wait_ge(xn_ready, count)
                    src = ps[0:C, :].rearrange("p (row win col) -> p row win col", row=WS, win=WS)
                    dst = y[0:C, c, :].rearrange("p (win row col) -> p row win col", win=WS, row=WS)
                    nc.scalar.activation(dst, src, ACT.Identity, bias=l0sc[:, 0:1],
                                         scale=col97(V97 + 1)).then_inc(misc_evac, 1)
                    act.wait_ge(misc_evac, n + 1)
                    nc.scalar.activation(ysq[:, c % 2, :], y[0:C, c, :], ACT.Square).then_inc(ysq_ready, 1)
                elif kind == "ssq":
                    bi, c = job[1:]
                    if c % 4 == 0:
                        if due(count := 2 * bi + c // 4):
                            act.wait_ge(inv_ready, count)
                    nc.scalar.activation(ssq[:, (c % 4) * PPC:(c % 4 + 1) * PPC], ps[:, 0:PPC],
                                         ACT.Copy).then_inc(misc_evac, 1)
                elif kind == "inv":
                    bi, c = job[1:]
                    if due(count := CHUNKS * bi + c - 1):
                        act.wait_ge(xn_ready, count)
                    nc.scalar.activation(invb[:, c % 2, :], ps[0:C + 1, :], ACT.Copy).then_inc(misc_evac, 1)
                elif kind == "fc2":
                    bc, c = job[1:]
                    src = ps[0:C, :].rearrange("p (win row col) -> p win row col", win=WS, row=WS)
                    dst = x1[:, c * WS:(c + 1) * WS, :].rearrange("p row (win col) -> p win row col", win=WS)
                    nc.scalar.activation(dst, src, ACT.Identity, bias=l0sc[:, 1:2]).then_inc(misc_evac, 1)
                elif kind == "w1":
                    t, s, (gr, m) = job[1:]
                    if m == 0:
                        if due(count := tap_number(s - 1, gr, TAPS - 1)):
                            act.wait_ge(tap_done, count)
                    sc, sh = sc1[:, gr:gr + 1], sh1[:, gr:gr + 1]
                    if gr < FULL:
                        r0, r1 = 6 * m, 6 * m + 6
                        if t == 0 and m == 0:
                            r0 = 1
                            nc.scalar.activation(hpad[:, gr, 0, 1:W + 1], zrow[:, :], ACT.Copy)
                        if t == STRIPS - 1 and m == 2:
                            r1 -= 1
                            nc.scalar.activation(hpad[:, gr, STRIP + 1, 1:W + 1], zrow[:, :], ACT.Copy)
                        o = (r0 - 6 * m) * W
                        nc.scalar.activation(hpad[:, gr, r0:r1, 1:W + 1],
                                             ps[:, o:o + (r1 - r0) * W].rearrange("p (row col) -> p row col", col=W),
                                             ACT.Relu, bias=sh, scale=sc).then_inc(misc_evac, 1)
                    else:
                        edge = 0 if (t == 0 and m == 0) else 1 if (t == STRIPS - 1 and m == 1) else None
                        if edge is None:
                            nc.scalar.activation(hpad[:, gr, 5 * m:5 * m + 5, 1:W + 1],
                                                 ps[:, 0:5 * W].rearrange("p (row col) -> p row col", col=W),
                                                 ACT.Relu, bias=sh, scale=sc).then_inc(misc_evac, 1)
                        else:
                            zr = 9 * edge
                            h = 64 * edge
                            nc.scalar.activation(hpad[h:h + 64, gr, zr, 1:W + 1], zrow[h:h + 64, :], ACT.Copy)
                            for u in range(2):
                                r0, r1 = 5 * m, 5 * m + 5
                                if u == edge:
                                    r0, r1 = (1, 5) if edge == 0 else (5, 9)
                                o = (r0 - 5 * m) * W
                                h = 64 * u
                                last = nc.scalar.activation(
                                    hpad[h:h + 64, gr, r0:r1, 1:W + 1],
                                    ps[h:h + 64, o:o + (r1 - r0) * W].rearrange("p (row col) -> p row col", col=W),
                                    ACT.Relu, bias=sh[h:h + 64, :], scale=sc[h:h + 64, :])
                            last.then_inc(misc_evac, 1)
                else:
                    t, s, q = job[1:]
                    cc = q // 2
                    if q % 2 == 0:
                        if due(count := 16 * s):
                            act.wait_ge(store_done[cc], count)
                    nc.scalar.activation(res[:, cc, (q % 2) * 4 * W:(q % 2 + 1) * 4 * W], ps[0:C, 0:4 * W],
                                         ACT.Identity, bias=sc2[:, 1:2]).then_inc(misc_evac, 1)

            def featT_copy(P, p):
                act.wait_ge(featT_ready, P + 1)
                if due(count := P - 1):
                    act.wait_ge(onehot_in, count)
                nc.scalar.activation(featT[:, p % 2, :], pself[0:32, 256:320], ACT.Copy).then_inc(featT_evac, 1)

            def feature_square(P, p):
                act.wait_ge(a_ready, P + 1)
                nc.scalar.activation(feat[:, p % 2, 1, :], feat[:, p % 2, 0, :], ACT.Square).then_inc(feat_ready, 1)

            def onehot(P, p):
                act.wait_ge(onehot_in, P + 1)
                if due(count := P - 1):
                    act.wait_ge(self_ready, count)
                for w in range(2):
                    h = 64 * w
                    last = nc.scalar.activation(MV[h:h + 64, p % 2, w, 0:KN, :], pone[h:h + 64, :, :], ACT.Relu,
                                                bias=nbias[h:h + 64, :], scale=1.0)
                last.then_inc(onehot_ready, 1)

            def vu_copy(P, p):
                act.wait_ge(vu_ready, P + 1)
                r = p % 2
                nc.scalar.activation(VU[:, r, :, :], pvu[:, 0:2 * O].rearrange("p (win o) -> p win o", win=2),
                                     ACT.Copy).then_inc(vu_evac, 1)

            def gelu(P, p, part):
                act.wait_ge(gather_ready, 3 * P + part + 1)
                if part == 0:
                    if due(count := P - 1):
                        act.wait_ge(hid_ready, count)
                nc.scalar.activation(g[:, p % 2, part, 0:KN, :],
                                     pg[(3 * p + part) % 2][:, :].rearrange("p (k n) -> p k n", k=KN),
                                     ACT.Gelu).then_inc(gelu_done, 1)

            def gelu_self(P, p):
                act.wait_ge(self_ready, P + 1)
                nc.scalar.activation(g[:, p % 2, :, KN, :],
                                     pself[:, 0:192].rearrange("p (c n) -> p c n", c=3),
                                     ACT.Gelu).then_inc(self_gelu, 1)

            def tap0(b, p, o, t, gr):
                m = 2 if gr < FULL else 1
                fb, fp = when(b, p, o - w1_slot(gr, m))
                act.wait_ge(misc_evac, job_at(fb, fp, "w1", (gr, m)))
                rows = STRIP if gr < FULL else STRIP // 2
                nc.scalar.activation(acc[:, t % 2, gr, 0:rows * W].rearrange("p (row col) -> p row col", col=W),
                                     hpad[:, gr, 0:rows, 0:W], ACT.Copy, scale=wd[:, gr, 0:1]).then_inc(tap0_done, 1)

            def relu2(s, par, gr):
                if due(count := tap_number(s, gr, TAPS - 1)):
                    act.wait_ge(tap_done, count)
                n = STRIP * W if gr < FULL else STRIP * W // 2
                nc.scalar.activation(acc[:, par, gr, 0:n], acc[:, par, gr, 0:n], ACT.Relu,
                                     bias=shd[:, gr:gr + 1], scale=scd[:, gr:gr + 1]).then_inc(relu_done, 1)

            def diagonals(bi, c):
                act.wait_ge(inv_ready, 2 * bi + c // 4 + 1)
                for j in range(PPC):
                    k = (c % 4) * PPC + j
                    last = nc.scalar.activation(diag[:, c % 2, j, :], eye128[:, :], ACT.Copy, scale=inv[:, k:k + 1])
                last.then_inc(diag_ready, 1)

            act.wait_ge(bn_sqrt_in, 4)
            nc.scalar.activation(v2_row, v2_row, ACT.Sqrt).then_inc(bn_sqrt_out, 1)
            nc.scalar.activation(bn[:, 0:2, :], bn[:, 0:2, :], ACT.Sqrt).then_inc(bn_sqrt_out, 1)
            nc.scalar.activation(tmp2[:, 0:1], tmp2[:, 0:1], ACT.Sqrt).then_inc(bn_sqrt_out, 1)
            act.wait_ge(consts_ready, 1)

            def image(b, p0, p1):
                for p in range(p0, p1):
                    P = PAIRS * b + p
                    if isinstance(b, int) and b == -1 and p == 16 + NORMS_AT:
                        act.wait_ge(consts_ready, 2)
                    jobs = misc_jobs(b, p)
                    h = 1 if p < 16 else 0
                    bi = b if h else b + 1
                    if valid(P, NPAIRS):
                        gelu(P, p, 0)
                    for k in part_of(jobs, 0):
                        shared_evac(b, p, k, jobs[k])
                    for o, t, s, groups in due_in(TAP0_AT, b, p):
                        for gr in groups:
                            tap0(b, p, o, t, gr)
                    if valid(P + 1, NPAIRS):
                        onehot(P + 1, p + 1)
                    if valid(P + 2, NPAIRS):
                        featT_copy(P + 2, p + 2)
                    if valid(P, NPAIRS):
                        gelu(P, p, 1)
                    for k in part_of(jobs, 1):
                        shared_evac(b, p, k, jobs[k])
                    if p % 16 in DIAG_AT and valid(bi, B):
                        diagonals(bi, 4 * h + DIAG_AT[p % 16])
                    if valid(P + 1, NPAIRS):
                        vu_copy(P + 1, p + 1)
                    if valid(P, NPAIRS):
                        gelu(P, p, 2)
                    if valid(P + 3, NPAIRS):
                        feature_square(P + 3, p + 3)
                    for k in part_of(jobs, 2):
                        shared_evac(b, p, k, jobs[k])
                    if valid(P, NPAIRS):
                        gelu_self(P, p)
                    for k in part_of(jobs, 3):
                        shared_evac(b, p, k, jobs[k])
                    for o, t, s, groups in due_in(TAP0_LATE, b, p):
                        for gr in groups:
                            tap0(b, p, o, t, gr)
                    for _, t, s, groups in due_in(RELU2_AT, b, p):
                        for gr in groups:
                            relu2(s, t % 2, gr)

            image_loop(act, image, TAIL)

        @block.vector
        def _(dve):
            steps = [0]

            def step(ins):
                steps[0] += 1
                ins.then_inc(dve_setup, 1)
                dve.wait_ge(dve_setup, steps[0])

            nc.vector.memset(ones[:, :], 1.0)
            nc.vector.memset(y[C:C + 1, :, :], 1.0)
            dve.wait_ge(w97_load, 16)
            for k, v in ((0, V97), (1, V97 + 3)):
                step(nc.vector.tensor_tensor(l0sc[:, k:k + 1], col97(v), col97(v + 1), ALU.mult))
                step(nc.vector.tensor_tensor(l0sc[:, k:k + 1], l0sc[:, k:k + 1], col97(v + 2), ALU.add))
            dve.sem_inc(consts_ready, 1)
            nc.vector.memset(hpad[:, :, :, 0:1], 0.0)
            nc.vector.memset(hpad[:, :, :, W + 1:PADW], 0.0)
            nc.vector.memset(zrow[:, :], 0.0)
            nc.vector.memset(expo[:, :], -0.5)
            nc.vector.memset(onesq[:, :, :], 1.0)
            dve.wait_ge(param_load, 80)
            EPS = 1e-5
            nc.vector.tensor_scalar(bn[:, 0, :], bnp[:, 3, :], EPS, None, ALU.add).then_inc(bn_sqrt_in, 1)
            nc.vector.tensor_scalar(bn[:, 1, :], bnp[:, 7, :], EPS, None, ALU.add).then_inc(bn_sqrt_in, 1)
            nc.vector.tensor_scalar(tmp2[:, 0:1], col97(V97 + 9), EPS, None, ALU.add).then_inc(bn_sqrt_in, 1)
            nc.vector.tensor_scalar(v2_row, v2_row, EPS, None, ALU.add).then_inc(bn_sqrt_in, 1)
            step(nc.vector.tensor_copy(c16[:, :], c16f[:, :]))
            for r in range(2):
                for w in range(2):
                    v, u = 64 * w, 64 * (1 - w)
                    nc.vector.tensor_copy(MV[v:v + 64, r, w, KN, :], eye[v:v + 64, :])
                    step(nc.vector.tensor_copy(MV[u:u + 64, r, w, :, :],
                                               eye[u:u + 64, :].unsqueeze(1).to_broadcast([64, KN + 1, NODES])))
            es = r97[:, 0:O]
            step(nc.vector.tensor_tensor(wVU[:, 1, :], r97[:, O:2 * O], r97[:, 2 * O:3 * O], ALU.subtract))
            step(nc.vector.tensor_tensor(wVU[:, 1, :], wVU[:, 1, :], es, ALU.mult))
            step(nc.vector.tensor_tensor(wVU[:, 0, :], r97[:, 2 * O:3 * O], es, ALU.mult))
            step(nc.vector.tensor_tensor(wVU[C:C + 1, 1, :], wVU[C:C + 1, 1, :],
                                         w97[C:C + 1, 0:O], ALU.add))
            dve.wait_ge(bn_sqrt_out, 3)
            step(nc.vector.reciprocal(bn[:, 0:2, :], bn[:, 0:2, :]))
            step(nc.vector.reciprocal(tmp2[:, 0:1], tmp2[:, 0:1]))
            for k, (sc, sh) in enumerate(((sc1, sh1), (scd, shd))):
                step(nc.vector.tensor_tensor(sc[:, :], bnp[:, 4 * k, :], bn[:, k, :], ALU.mult))
                step(nc.vector.tensor_tensor(sh[:, :], bnp[:, 4 * k + 2, :], sc[:, :], ALU.mult))
                step(nc.vector.tensor_tensor(sh[:, :], bnp[:, 4 * k + 1, :], sh[:, :], ALU.subtract))
            step(nc.vector.reciprocal(v2_row, v2_row))
            step(nc.vector.tensor_tensor(g2_row, g2_row, v2_row, ALU.mult))
            step(nc.vector.tensor_tensor(fc2T, fc2T, fc2s_row.unsqueeze(1).to_broadcast([128, 3, C]), ALU.mult))
            step(nc.vector.tensor_tensor(w2T, w2T, g2_row.unsqueeze(1).to_broadcast([128, 5, C]), ALU.mult))
            step(nc.vector.tensor_tensor(sc2[:, 0:1], col97(V97 + 6), tmp2[:, 0:1], ALU.mult))
            step(nc.vector.tensor_tensor(sc2[:, 1:2], col97(V97 + 8), sc2[:, 0:1], ALU.mult))
            nc.vector.tensor_tensor(sc2[:, 1:2], col97(V97 + 7), sc2[:, 1:2], ALU.subtract).then_inc(consts_ready, 1)

            def largest(P, p):
                if due(count := P + 1):
                    dve.wait_ge(score_ready, count)
                dve.sem_inc(dve_passed, 1)
                nc.vector.max(top8[:, p % 2, :], pscore[:, 0:NODES]).then_inc(top8_ready, 1)

            def indices(P, p):
                r = p % 2
                if due(count := P + 1):
                    dve.wait_ge(top8_ready, count)
                dve.sem_inc(dve_passed, 1)
                nc.vector.max_index(idx[:, r, :], top8[:, r, :], pscore[:, 0:NODES]).then_inc(idx_ready, 1)

            def feature_a(P, p):
                r = p % 2
                if due(count := P + 1):
                    dve.wait_ge(idx_ready, count)
                if due(count := P - 1):
                    dve.wait_ge(featT_ready, count)
                nc.vector.scalar_tensor_tensor(out=feat[:, r, 0, :].rearrange("p (win k) -> p win k", win=2),
                                               in0=idx[:, r, :].unsqueeze(1).to_broadcast([128, 2, KN]),
                                               scalar=-32.0, in1=maskw, op0=ALU.add, op1=ALU.mult).then_inc(a_ready, 1)

            def normalise(b, p, bi, c):
                fb, fp = when(b, p, 1)
                if due(count := job_at(fb, fp, "inv", c)):
                    dve.wait_ge(misc_evac, count)
                if due(count := PAIRS * (bi - 1) + PPC * (c + 1)):
                    dve.wait_ge(score_ready, count)
                nc.vector.tensor_tensor(xn[:, c, :], y[:, c, :], invb[:, c % 2, :], ALU.mult).then_inc(xn_ready, 1)

            def maxima(P, p):
                c, j, r = (p % PAIRS) // PPC, p % PPC, p % 2
                if due(count := P + 1):
                    dve.wait_ge(self_gelu, count)
                nc.vector.tensor_reduce(hid[:, c % 2, j, :, :], g[:, r].rearrange("p c k n -> p c n k"),
                                        op=ALU.max, axis=AX.X).then_inc(hid_ready, 1)

            def tap(s, sp_, gr, k):
                dy, dx = k // 3, k % 3
                n = STRIP if gr < FULL else STRIP // 2
                src = hpad[:, gr, dy:dy + n, dx:dx + W]
                dst = acc[:, sp_, gr, 0:n * W].rearrange("p (row col) -> p row col", col=W)
                wk = wd[:, gr, k:k + 1]
                if k == 1:
                    dve.wait_ge(tap0_done, 5 * s + gr + 1)
                else:
                    dve.wait_ge(tap_done, tap_number(s, gr, k - 1))
                nc.vector.scalar_tensor_tensor(out=dst, in0=src, scalar=wk, in1=dst, op0=ALU.mult,
                                               op1=ALU.add).then_inc(tap_done, 1)

            def image(b, p0, p1):
                for p in range(p0, p1):
                    P = PAIRS * b + p
                    taps = [(s, t % 2, gr, k) for _, t, s, entries in due_in(TAP_AT, b, p) for gr, k in entries]
                    new = valid(P + 3, NPAIRS)
                    h = 1 if p < 16 else 0
                    bi = b if h else b + 1
                    for a in taps[0:2]:
                        tap(*a)
                    if new:
                        largest(P + 3, p + 3)
                    if p % 16 in XN_AT and valid(bi, B):
                        normalise(b, p, bi, 4 * h + XN_AT[p % 16])
                    for a in taps[2:3]:
                        tap(*a)
                    if new:
                        indices(P + 3, p + 3)
                    for a in taps[3:4]:
                        tap(*a)
                    if new:
                        feature_a(P + 3, p + 3)
                    if valid(P - 1, NPAIRS):
                        maxima(P - 1, p - 1)
                    for a in taps[4:]:
                        tap(*a)

            image_loop(dve, image, TAIL)


TAIL = SLOTS + max(STORE_AT) + 1
P97 = C + HID + 12
P128 = 11 * C + 45 + 40
CF = 81 + NODES
C16 = 256 + KN * 128


def kernel(**inputs):
    import numpy as np
    import concourse.bacc as bacc
    from concourse.bass_utils import run_bass_kernel_spmd as run

    f = {k: np.ascontiguousarray(v) for k, v in inputs.items()}

    def l0(n):
        return f["L0_conv_" + n]

    def l1(n):
        return f["L1_conv_" + n]

    def grouped(v):
        v = v.reshape(HID, -1)
        full = v[:FULL * 128].reshape(FULL, 128, -1).transpose(1, 0, 2)
        half = np.concatenate([v[FULL * 128:]] * 2, 0)[:, None, :]
        return np.concatenate([full, half], 1)

    p97 = np.zeros((C + 1, P97), np.float32)
    p97[:C, :C] = l0("fc1_w").T
    p97[:C, C:C + HID] = l1("w1").T
    p97[C, :O] = l0("et")
    names = [l0("fc1_b"), l0("fc1_s"), l0("fc1_t"), l0("fc2_b"), l0("fc2_s"), l0("fc2_t"),
             l1("g2"), l1("b2"), l1("m2"), l1("v2")]
    for k, v in enumerate(names):
        p97[:C, C + HID + k] = v
    fc2T = l0("fc2_w").T
    zeros = np.zeros((O - ONE128, C), np.float32)
    p128 = np.concatenate([
        fc2T[:ONE128], np.concatenate([fc2T[ONE128:], zeros], 0), np.concatenate([zeros, fc2T[ONE128:]], 0),
        grouped(l1("w2").T).reshape(128, -1), grouped(l1("wd")).reshape(128, -1),
    ] + [grouped(l1(n)).reshape(128, 5) for n in ("g1", "b1", "m1", "v1", "gd", "bd", "md", "vd")]
        + [np.broadcast_to(v, (128, C)) for v in (l0("fc2_s"), l1("g2"), l1("v2"))], 1)
    ewT = l0("ew").T
    rows97 = np.zeros((C + 1, 3 * O), np.float32)
    rows97[:, :O] = l0("es")
    rows97[:C, O:2 * O] = ewT[:C]
    rows97[C, O:2 * O] = l0("eb")
    rows97[:C, 2 * O:] = ewT[C:]
    j = np.arange(128) % NODES - 32
    eye = np.eye(NODES, dtype=np.float32)
    cst = np.zeros((128, CF), np.float32)
    cst[:, 0] = 1 - j * j
    cst[:64, 1:9] = 1
    cst[64:, 9:17] = 1
    cst[:, 17:81] = 1
    cst[:, 81:] = np.concatenate([eye, eye], 0)
    c16 = np.zeros((128, C16), np.float32)
    c16[:, 0:64] = np.concatenate([eye, eye], 0)
    c16[:64, 64:192] = np.concatenate([eye, eye], 1)
    c16[:64, 192:256] = -8 * eye
    lk = np.zeros((2, 2, KN, KN, 2, NODES), np.float32)
    for w in range(2):
        for k in range(KN):
            lk[0, w, k, k, w] = 2 * j[:NODES]
            lk[1, w, k, k, w] = -1
    c16[:32, 256:] = lk.reshape(32, -1)

    arrays = {"x": f["x"], "p97": p97, "p128": np.ascontiguousarray(p128), "rows97": rows97, "consts": cst,
              "consts128": np.eye(128, dtype=np.float32), "consts16": c16}
    nc = bacc.Bacc("TRN2", target_bir_lowering=False, num_devices=1)
    args = [nc.dram_tensor(f"in_{n}_dram", a.shape, mybir.dt.from_np(a.dtype), kind="ExternalInput").ap()
            for n, a in arrays.items()]
    out = nc.dram_tensor("out_0_dram", f["x"].shape, mybir.dt.float32, kind="ExternalOutput").ap()
    build(nc, *args, out)
    r = run(nc, [{f"in_{n}_dram": a for n, a in arrays.items()}], core_ids=[0])
    return r.results[0]["out_0_dram"]
```
